# Optimizing a Trainium2 kernel written in Bass

```python
import numpy as np
import jax
import jax.numpy as jnp

def _softmax(x, axis=-1):
    return jax.nn.softmax(x, axis=axis)

def _gelu(x):
    return jax.nn.gelu(x, approximate=True)

def _silu(x):
    return jax.nn.silu(x)

def _sigmoid(x):
    return jax.nn.sigmoid(x)

def _layernorm(x, axis=-1, eps=1e-05):
    m = jnp.mean(x, axis=axis, keepdims=True)
    v = jnp.var(x, axis=axis, keepdims=True)
    return (x - m) / jnp.sqrt(v + eps)

def _scatter_add(tgt, idx, src, axis=0):
    return tgt.at[idx].add(src)

def _segment_sum(src, seg, n):
    return jax.ops.segment_sum(src, seg, n)
kernel_name = 'mk_gnn_resnorm_d4_gnn_r8_7c959f'

def setup_inputs(seed: int=0):
    np.random.seed(seed)
    _w = jnp.asarray

    def _rec_inputs():
        import jax
        import jax.numpy as jnp
        _gk = jax.random.key(seed)
        x = -0.0003713 + 1 * jax.random.normal(jax.random.fold_in(_gk, 1), (6250, 128), jnp.float32)
        _s = jax.random.randint(jax.random.fold_in(_gk, 2), (50000,), 0, 6250, jnp.int32)
        _d = jax.random.randint(jax.random.fold_in(_gk, 3), (50000,), 0, 6250, jnp.int32)
        _loop = jnp.arange(6250, dtype=jnp.int32)
        src = jnp.concatenate([_s, _d, _loop])
        dst = jnp.concatenate([_d, _s, _loop])
        _o = jnp.argsort(dst, stable=True)
        src = src[_o]
        dst = dst[_o]
        edge_attr_128 = -5.16925e-05 + 1.00005 * jax.random.normal(jax.random.fold_in(_gk, 12), (106250, 128), jnp.float32)
        edge_attr_50 = jax.random.uniform(jax.random.fold_in(_gk, 13), (106250, 50), jnp.float32, 0.0, 1)
        edge_weight = jax.random.uniform(jax.random.fold_in(_gk, 15), (106250,), jnp.float32, 0.0, 0.999999)
        edge_weight_n2 = jax.random.uniform(jax.random.fold_in(_gk, 16), (106250,), jnp.float32, 0.0, 0.999999)
        return (x, src, dst, edge_attr_128, edge_attr_50, edge_weight, edge_weight_n2)
    x, src, dst, edge_attr_128, edge_attr_50, edge_weight, edge_weight_n2 = _rec_inputs()

    def _L0_gnn_setup():
        import jax, jax.numpy as jnp
        import numpy as np
        ALPHA = 0.2
        EPS = 1e-08
        N_NODES = 12500
        N_EDGES = 200000
        D_IN = 128
        D_OUT = 128
        key = jax.random.key(seed)
        k1, k2, k3, k4, k5 = jax.random.split(key, 5)
        h = jax.random.normal(k1, (N_NODES, D_IN), dtype=jnp.float32)
        edge_index = jax.random.randint(k2, (2, N_EDGES), 0, N_NODES, dtype=jnp.int32)
        edge_weight = jax.random.uniform(k3, (N_EDGES,), dtype=jnp.float32)
        W = jax.random.normal(k4, (D_OUT, D_IN), dtype=jnp.float32) * (1.0 / np.sqrt(D_IN))
        a = jax.random.normal(k5, (1, 2 * D_OUT), dtype=jnp.float32) * (1.0 / np.sqrt(2 * D_OUT))
        return {'h': h, 'edge_index': edge_index, 'edge_weight': edge_weight, 'W': W, 'a': a}
    _L0_gnn_all = _L0_gnn_setup()
    _L0_gnn_in = {k: v for k, v in _L0_gnn_all.items() if k in ('W', 'a')}
    del _L0_gnn_all

    def _L1_gnn_setup():
        import jax, jax.numpy as jnp
        import numpy as np
        N_NODES = 6250
        N_EDGES = 100000
        D = 128
        key = jax.random.key(seed)
        k = jax.random.split(key, 7)
        scale = 1.0 / np.sqrt(D)
        return {'x': jax.random.normal(k[0], (N_NODES, D), dtype=jnp.float32), 'adj_vals': jax.random.uniform(k[1], (N_EDGES,), dtype=jnp.float32), 'adj_mask': jnp.ones((N_EDGES,), dtype=jnp.float32), 'W0': jax.random.normal(k[2], (D, D), dtype=jnp.float32) * scale, 'W1': jax.random.normal(k[3], (D, D), dtype=jnp.float32) * scale, 'edge_src': jax.random.randint(k[4], (N_EDGES,), 0, N_NODES, dtype=jnp.int32), 'edge_dst': jax.random.randint(k[5], (N_EDGES,), 0, N_NODES, dtype=jnp.int32)}
    _L1_gnn_all = _L1_gnn_setup()
    _L1_gnn_in = {k: v for k, v in _L1_gnn_all.items() if k in ('W0', 'W1')}
    del _L1_gnn_all

    def _L2_gnn_setup():
        import jax, jax.numpy as jnp
        import numpy as np
        N_NODES = 6250
        N_EDGES = 100000
        D_MODEL = 128
        N_HEADS = 8
        HEAD_DIM = D_MODEL // N_HEADS
        SCALE = 1.0 / np.sqrt(HEAD_DIM)

        def _linear_params(key, d_in, d_out):
            kw, kb = jax.random.split(key)
            bound = 1.0 / np.sqrt(d_in)
            W = jax.random.uniform(kw, (d_in, d_out), jnp.float32, -bound, bound)
            b = jax.random.uniform(kb, (d_out,), jnp.float32, -bound, bound)
            return (W, b)
        key = jax.random.key(seed)
        ks = jax.random.split(key, 8)
        node_features = jax.random.normal(ks[0], (N_NODES, D_MODEL), jnp.float32)
        edge_index = jax.random.randint(ks[1], (2, N_EDGES), 0, N_NODES, jnp.int64 if jax.config.jax_enable_x64 else jnp.int32)
        edge_features = jax.random.normal(ks[2], (N_EDGES, D_MODEL), jnp.float32)
        Wq, bq = _linear_params(ks[3], D_MODEL, D_MODEL)
        Wk, bk = _linear_params(ks[4], D_MODEL, D_MODEL)
        Wv, bv = _linear_params(ks[5], D_MODEL, D_MODEL)
        We, be = _linear_params(ks[6], D_MODEL, N_HEADS)
        Wo, bo = _linear_params(ks[7], D_MODEL, D_MODEL)
        return {'node_features': node_features, 'edge_index': edge_index, 'edge_features': edge_features, 'Wq': Wq, 'bq': bq, 'Wk': Wk, 'bk': bk, 'Wv': Wv, 'bv': bv, 'We': We, 'be': be, 'Wo': Wo, 'bo': bo}
    _L2_gnn_all = _L2_gnn_setup()
    _L2_gnn_in = {k: v for k, v in _L2_gnn_all.items() if k in ('Wq', 'bq', 'Wk', 'bk', 'Wv', 'bv', 'We', 'be', 'Wo', 'bo')}
    del _L2_gnn_all

    def _L3_gnn_setup():
        import jax, jax.numpy as jnp
        import numpy as np
        N_NODES = 5000
        N_EDGES = 80000
        HIDDEN = 128
        FILTERS = 128
        NG = 50

        def _mlp_params(key, d_in, d_mid, d_out):
            k1, k2 = jax.random.split(key)
            s1 = 1.0 / np.sqrt(d_in)
            s2 = 1.0 / np.sqrt(d_mid)
            return (jax.random.uniform(k1, (d_in, d_mid), jnp.float32, -s1, s1), jnp.zeros((d_mid,), jnp.float32), jax.random.uniform(k2, (d_mid, d_out), jnp.float32, -s2, s2), jnp.zeros((d_out,), jnp.float32))
        key = jax.random.key(seed)
        ks = jax.random.split(key, 6)
        h = jax.random.normal(ks[0], (N_NODES, HIDDEN), jnp.float32)
        edge_index = jax.random.randint(ks[1], (2, N_EDGES), 0, N_NODES, jnp.int64)
        dist_feat = jax.random.uniform(ks[2], (N_EDGES, NG), jnp.float32)
        fw1, fb1, fw2, fb2 = _mlp_params(ks[3], NG, FILTERS, FILTERS)
        aw1, ab1, aw2, ab2 = _mlp_params(ks[4], HIDDEN, FILTERS, FILTERS)
        ow1, ob1, ow2, ob2 = _mlp_params(ks[5], FILTERS, HIDDEN, HIDDEN)
        return {'h': h, 'edge_index': edge_index, 'dist_feat': dist_feat, 'fw1': fw1, 'fb1': fb1, 'fw2': fw2, 'fb2': fb2, 'aw1': aw1, 'ab1': ab1, 'aw2': aw2, 'ab2': ab2, 'ow1': ow1, 'ob1': ob1, 'ow2': ow2, 'ob2': ob2}
    _L3_gnn_all = _L3_gnn_setup()
    _L3_gnn_in = {k: v for k, v in _L3_gnn_all.items() if k in ('fw1', 'fb1', 'fw2', 'fb2', 'aw1', 'ab1', 'aw2', 'ab2', 'ow1', 'ob1', 'ow2', 'ob2')}
    del _L3_gnn_all
    return {'x': x, 'src': src, 'dst': dst, 'edge_attr_128': edge_attr_128, 'edge_attr_50': edge_attr_50, 'edge_weight': edge_weight, 'edge_weight_n2': edge_weight_n2, 'L0_gnn_W': _L0_gnn_in['W'], 'L0_gnn_a': _L0_gnn_in['a'], 'L1_gnn_W0': _L1_gnn_in['W0'], 'L1_gnn_W1': _L1_gnn_in['W1'], 'L2_gnn_Wq': _L2_gnn_in['Wq'], 'L2_gnn_bq': _L2_gnn_in['bq'], 'L2_gnn_Wk': _L2_gnn_in['Wk'], 'L2_gnn_bk': _L2_gnn_in['bk'], 'L2_gnn_Wv': _L2_gnn_in['Wv'], 'L2_gnn_bv': _L2_gnn_in['bv'], 'L2_gnn_We': _L2_gnn_in['We'], 'L2_gnn_be': _L2_gnn_in['be'], 'L2_gnn_Wo': _L2_gnn_in['Wo'], 'L2_gnn_bo': _L2_gnn_in['bo'], 'L3_gnn_fw1': _L3_gnn_in['fw1'], 'L3_gnn_fb1': _L3_gnn_in['fb1'], 'L3_gnn_fw2': _L3_gnn_in['fw2'], 'L3_gnn_fb2': _L3_gnn_in['fb2'], 'L3_gnn_aw1': _L3_gnn_in['aw1'], 'L3_gnn_ab1': _L3_gnn_in['ab1'], 'L3_gnn_aw2': _L3_gnn_in['aw2'], 'L3_gnn_ab2': _L3_gnn_in['ab2'], 'L3_gnn_ow1': _L3_gnn_in['ow1'], 'L3_gnn_ob1': _L3_gnn_in['ob1'], 'L3_gnn_ow2': _L3_gnn_in['ow2'], 'L3_gnn_ob2': _L3_gnn_in['ob2']}

def reference(x, src, dst, edge_attr_128, edge_attr_50, edge_weight, edge_weight_n2, L0_gnn_W, L0_gnn_a, L1_gnn_W0, L1_gnn_W1, L2_gnn_Wq, L2_gnn_bq, L2_gnn_Wk, L2_gnn_bk, L2_gnn_Wv, L2_gnn_bv, L2_gnn_We, L2_gnn_be, L2_gnn_Wo, L2_gnn_bo, L3_gnn_fw1, L3_gnn_fb1, L3_gnn_fw2, L3_gnn_fb2, L3_gnn_aw1, L3_gnn_ab1, L3_gnn_aw2, L3_gnn_ab2, L3_gnn_ow1, L3_gnn_ob1, L3_gnn_ow2, L3_gnn_ob2):
    import jax
    import jax.numpy as jnp

    def _L0_gnn_ref(h, edge_index, edge_weight, W, a):
        import jax, jax.numpy as jnp
        import numpy as np
        ALPHA = 0.2
        EPS = 1e-08
        N_NODES = 12500
        N_EDGES = 200000
        D_IN = 128
        D_OUT = 128
        num_nodes = h.shape[0]
        Wh = h @ W.T
        src, dst = (edge_index[0], edge_index[1])
        d_out = Wh.shape[1]
        a_src = a[0, :d_out]
        a_dst = a[0, d_out:]
        Wh_src = Wh[src]
        e = Wh_src @ a_src + Wh[dst] @ a_dst
        e = jnp.where(e >= 0, e, ALPHA * e)
        e = e * edge_weight
        seg_max = jax.ops.segment_max(e, dst, num_segments=num_nodes)
        seg_max = jnp.maximum(seg_max, 0.0)
        ex = jnp.exp(e - seg_max[dst])
        seg_sum = jax.ops.segment_sum(ex, dst, num_segments=num_nodes)
        att = ex / (seg_sum[dst] + EPS)
        h_prime = jax.ops.segment_sum(att[:, None] * Wh_src, dst, num_segments=num_nodes)
        return h_prime

    def _L1_gnn_ref(x, adj_vals, adj_mask, W0, W1, edge_src, edge_dst):
        import jax, jax.numpy as jnp
        import numpy as np
        N_NODES = 6250
        N_EDGES = 100000
        D = 128
        vals = adj_vals * adj_mask
        n = x.shape[0]

        def spmm(h):
            return jax.ops.segment_sum(h[edge_src] * vals[:, None], edge_dst, num_segments=n)
        h = spmm(x) @ W0.T
        h = jax.nn.relu(h)
        h = spmm(h) @ W1.T
        return h

    def _L2_gnn_ref(node_features, edge_index, edge_features, Wq, bq, Wk, bk, Wv, bv, We, be, Wo, bo):
        import jax, jax.numpy as jnp
        import numpy as np
        N_NODES = 6250
        N_EDGES = 100000
        D_MODEL = 128
        N_HEADS = 8
        HEAD_DIM = D_MODEL // N_HEADS
        SCALE = 1.0 / np.sqrt(HEAD_DIM)

        def _linear_params(key, d_in, d_out):
            kw, kb = jax.random.split(key)
            bound = 1.0 / np.sqrt(d_in)
            W = jax.random.uniform(kw, (d_in, d_out), jnp.float32, -bound, bound)
            b = jax.random.uniform(kb, (d_out,), jnp.float32, -bound, bound)
            return (W, b)
        N = node_features.shape[0]
        Q = (node_features @ Wq + bq).reshape(N, N_HEADS, HEAD_DIM)
        K = (node_features @ Wk + bk).reshape(N, N_HEADS, HEAD_DIM)
        V = (node_features @ Wv + bv).reshape(N, N_HEADS, HEAD_DIM)
        row, col = (edge_index[0], edge_index[1])
        scores = jnp.einsum('ehd,ehd->eh', Q[row], K[col]) * SCALE
        scores = scores + (edge_features @ We + be)
        seg_max = jax.ops.segment_max(scores, row, num_segments=N)
        seg_max = jnp.where(jnp.isfinite(seg_max), seg_max, 0.0)
        ex = jnp.exp(scores - seg_max[row])
        denom = jax.ops.segment_sum(ex, row, num_segments=N)
        att = ex / denom[row]
        out = jax.ops.segment_sum(att[:, :, None] * V[col], row, num_segments=N)
        out = out.reshape(N, D_MODEL)
        return out @ Wo + bo

    def _L3_gnn_ref(h, edge_index, dist_feat, fw1, fb1, fw2, fb2, aw1, ab1, aw2, ab2, ow1, ob1, ow2, ob2):
        import jax, jax.numpy as jnp
        import numpy as np
        N_NODES = 5000
        N_EDGES = 80000
        HIDDEN = 128
        FILTERS = 128
        NG = 50

        def _mlp_params(key, d_in, d_mid, d_out):
            k1, k2 = jax.random.split(key)
            s1 = 1.0 / np.sqrt(d_in)
            s2 = 1.0 / np.sqrt(d_mid)
            return (jax.random.uniform(k1, (d_in, d_mid), jnp.float32, -s1, s1), jnp.zeros((d_mid,), jnp.float32), jax.random.uniform(k2, (d_mid, d_out), jnp.float32, -s2, s2), jnp.zeros((d_out,), jnp.float32))
        silu = jax.nn.silu
        src, dst = (edge_index[0], edge_index[1])
        W = silu(dist_feat @ fw1 + fb1) @ fw2 + fb2
        x = silu(h @ aw1 + ab1) @ aw2 + ab2
        msg = W * x[src]
        agg = jax.ops.segment_sum(msg, dst, num_segments=h.shape[0])
        out = silu(agg @ ow1 + ob1) @ ow2 + ob2
        return h + out
    edge_index = jnp.stack([src, dst])
    x = _layernorm(x + _L0_gnn_ref(x, edge_index, edge_weight, L0_gnn_W, L0_gnn_a), axis=-1)
    x = _layernorm(x + _L1_gnn_ref(x, edge_weight, edge_weight_n2, L1_gnn_W0, L1_gnn_W1, src, dst), axis=-1)
    x = _layernorm(x + _L2_gnn_ref(x, edge_index, edge_attr_128, L2_gnn_Wq, L2_gnn_bq, L2_gnn_Wk, L2_gnn_bk, L2_gnn_Wv, L2_gnn_bv, L2_gnn_We, L2_gnn_be, L2_gnn_Wo, L2_gnn_bo), axis=-1)
    x = _layernorm(x + _L3_gnn_ref(x, edge_index, edge_attr_50, L3_gnn_fw1, L3_gnn_fb1, L3_gnn_fw2, L3_gnn_fb2, L3_gnn_aw1, L3_gnn_ab1, L3_gnn_aw2, L3_gnn_ab2, L3_gnn_ow1, L3_gnn_ob1, L3_gnn_ow2, L3_gnn_ob2), axis=-1)
    return x

_drawn_inputs = setup_inputs


def setup_inputs(seed=0):
    import zlib

    import numpy as np

    out = dict(_drawn_inputs(seed))
    spreads = {'L3_gnn_fb1': (0.0, 0.8),
     'L3_gnn_fb2': (0.0, 0.279),
     'L3_gnn_ab1': (0.0, 0.8),
     'L3_gnn_ab2': (0.0, 0.599),
     'L3_gnn_ob1': (0.0, 0.584),
     'L3_gnn_ob2': (0.0, 0.1)}
    factors = {'edge_attr_50': 8.0,
     'L2_gnn_Wq': 5.549,
     'L2_gnn_bq': 8.0,
     'L2_gnn_Wk': 5.603,
     'L2_gnn_bk': 64.0,
     'L2_gnn_be': 64.0,
     'edge_attr_128': 2.936,
     'L2_gnn_bv': 2.973,
     'L2_gnn_We': 2.846}
    for name, (base, spread) in spreads.items():
        noise = np.random.default_rng([zlib.crc32(name.encode()), seed]).standard_normal(out[name].shape)
        drawn = base * np.exp(spread * noise) if base else spread * noise
        out[name] = jnp.asarray(drawn.astype(out[name].dtype))
    for name, factor in factors.items():
        out[name] = (out[name] * factor).astype(out[name].dtype)
    return out
```

```python
import concourse.bass as bass
from concourse import mybir
from contextlib import ExitStack, contextmanager

P = 128
D = 128
N = 6250
E = 106250
NG = 50
NH, HD = 8, 16
NB = -(-N // P)
NN = NB * P
CH = 8
NC = 832
EP = P * NC
CHUNKS = NC // CH
FULLC = E // P
REST = E - P * FULLC
SLOTS = 4
PW = 64
SW = 16
W0 = 132
W2 = 144
KVW = D + NH * (HD + 1)
BIG = 1e30
GB = 7
GROUPS = NB // GB

F32, BF16, I32 = mybir.dt.float32, mybir.dt.bfloat16, mybir.dt.int32
ALU = mybir.AluOpType
ACT = mybir.ActivationFunctionType
AX = mybir.AxisListType


@contextmanager
def semaphores(nc):
    held = []

    def sem(name):
        held.append(nc.alloc_semaphore(name=name))
        return held[-1]

    yield sem
    nc.all_engine_barrier()
    nc.clear_and_free_semaphores(held)
    nc.all_engine_barrier()


def each(eng, total, slots, body, tail=0, head=True):
    rounds = (total - tail) // slots
    if head:
        for h in range(slots):
            body(0, h)
    with eng.Fori(1 if head else 0, rounds) as i:
        for h in range(slots):
            body(i, h)
    for k in range(rounds * slots, total):
        body(k // slots, k % slots)


def again(eng, sem, i, unit):
    if not (isinstance(i, int) and i == 0):
        eng.wait_ge(sem, i * unit)


def over(a, n):
    return a.unsqueeze(1).to_broadcast([a.shape[0], n, a.shape[1]])


def along(a, n):
    return a.unsqueeze(2).to_broadcast([a.shape[0], a.shape[1], n])


def gnn(nc, t, out):
    top = ExitStack()
    with top:
        def keep(name, shape, dt=F32):
            return top.enter_context(nc.sbuf_tensor(name, shape, dt))

        def dram(name, shape):
            return nc.dram_tensor(name, shape, F32, kind="Internal").ap()

        X = keep("X", [P, NB, D])
        ident = keep("ident", [P, P])
        identb = keep("identb", [P, P], BF16)
        later = keep("later", [P, P])
        iota = keep("iota", [P, P], BF16)
        part = keep("part", [P, 1])
        ones = keep("ones", [P, P])
        zeros = keep("zeros", [P, 256])
        base = [keep(f"base{k}", [P, NB]) for k in range(2)]
        count = [keep(f"count{k}", [P, NB]) for k in range(2)]
        has = [keep(f"has{k}", [P, NB]) for k in range(2)]
        endi = [keep(f"endi{k}", [P, NB + 2 * GB], I32) for k in range(2)]
        carryi = [keep(f"carryi{k}", [P, 1], I32) for k in range(2)]
        goes = [keep(f"goes{k}", [P, P]) for k in range(2)]
        goesT = [keep(f"goesT{k}", [P, P]) for k in range(2)]
        shut = [keep(f"shut{k}", [P, P]) for k in range(2)]
        ends = keep("ends", [P, W2])
        firsti = keep("firsti", [P, 1], I32)
        starti = keep("starti", [P, NB], I32)
        AD = keep("AD", [P, NB])

        NS = NC + 2 * CH
        src_d = keep("src_d", [P, NS], I32)
        meta_d = keep("meta_d", [P, NS, 5])
        dst_s = keep("dst_s", [P, NS], I32)
        src_s = keep("src_s", [P, NS], I32)
        meta_s = keep("meta_s", [P, NS, 2 + NH])

        w0 = keep("w0", [P, D + 2])
        w1 = [keep(f"w1_{k}", [P, D]) for k in range(2)]
        wq, wkv, we, wo = keep("wq", [P, D]), keep("wkv", [P, 2 * D]), keep("we", [P, NH]), keep("wo", [P, D])
        bq, bkv, bo = keep("bq", [1, D]), keep("bkv", [1, 2 * D]), keep("bo", [1, D])
        be = keep("be", [P, NH])
        fw1 = keep("fw1", [P, D])
        fw2, aw1, aw2, ow1, ow2 = (keep(n, [P, D]) for n in ("fw2", "aw1", "aw2", "ow1", "ow2"))
        fb1, ab1, ob1 = (keep(n, [P, 1]) for n in ("fb1", "ab1", "ob1"))
        fb2, ab2, ob2 = (keep(n, [1, D]) for n in ("fb2", "ab2", "ob2"))

        T0, T1, TQ = dram("T0", (NN, W0)), dram("T1", (NN, D)), dram("TQ", (NN, D))
        TH, T3, TKV = dram("TH", (NN, D)), dram("T3", (NN, D)), dram("TKV", (NN, KVW))
        ADT = dram("ADT", (NN, 1))
        sorted_d, sorted_s = dram("sorted_d", (EP, PW)), dram("sorted_s", (EP, SW))
        ADE = dram("ADE", (EP + P, 1))
        S0, S1, S2 = (dram(f"S{k}", (EP + P, w)) for k, w in enumerate((W0, D, W2)))

        def setup(inkeys):
            with semaphores(nc) as sem, ExitStack() as ctx:
                col_i = ctx.enter_context(nc.sbuf_tensor("col_i", [P, P], I32))
                part_i = ctx.enter_context(nc.sbuf_tensor("part_i", [P, 1], I32))
                colf = ctx.enter_context(nc.sbuf_tensor("colf", [P, P], F32))
                raw = ctx.enter_context(nc.sbuf_tensor("raw", [P, 3, D], F32))
                acol = ctx.enter_context(nc.sbuf_tensor("acol", [P, 2], F32))
                keys = [ctx.enter_context(nc.sbuf_tensor(f"keys{k}", [P, NC], I32)) for k in range(2)]
                cut = ctx.enter_context(nc.sbuf_tensor("cut", [P, NC], I32))
                ew2 = ctx.enter_context(nc.sbuf_tensor("ew2", [P, NC], F32))
                ew1 = ctx.enter_context(nc.sbuf_tensor("ew1", [P, NC], F32))
                psT = ctx.enter_context(nc.psum_tensor("psT", [P, 3, D], F32))
                psA = ctx.enter_context(nc.psum_tensor("psA", [P, 2], F32))
                iotas, cleared, loaded, consts, wT, w0T, a01 = (
                    sem(n)
                    for n in ("iotas", "cleared", "loaded", "consts", "wT", "w0T", "a01"))
                block = ctx.enter_context(nc.Block())
                loads = [
                    (X[:, 0:NB - 1, :], t["x"][0:(NB - 1) * P].rearrange("(b p) f -> p b f", p=P)),
                    (X[0:N - (NB - 1) * P, NB - 1, :], t["x"][(NB - 1) * P:N]),
                    (raw[:, 0, :], t["L0_gnn_W"]), (raw[:, 1, :], t["L1_gnn_W0"]), (raw[:, 2, :], t["L1_gnn_W1"]),
                    (acol[:, 0:1], t["L0_gnn_a"][0, 0:D].unsqueeze(1)),
                    (acol[:, 1:2], t["L0_gnn_a"][0, D:2 * D].unsqueeze(1)),
                    (wq[:, :], t["L2_gnn_Wq"]), (wkv[:, 0:D], t["L2_gnn_Wk"]), (wkv[:, D:2 * D], t["L2_gnn_Wv"]),
                    (we[:, :], t["L2_gnn_We"]), (wo[:, :], t["L2_gnn_Wo"]),
                    (bq[:, :], t["L2_gnn_bq"].unsqueeze(0)), (bkv[:, 0:D], t["L2_gnn_bk"].unsqueeze(0)),
                    (bkv[:, D:2 * D], t["L2_gnn_bv"].unsqueeze(0)), (bo[:, :], t["L2_gnn_bo"].unsqueeze(0)),
                    (be[:, :], t["L2_gnn_be"].unsqueeze(0).to_broadcast([P, NH])),
                    (fw1[4:4 + NG, :], t["L3_gnn_fw1"]), (fw1[PW + 4:PW + 4 + NG, :], t["L3_gnn_fw1"]),
                    (fw2[:, :], t["L3_gnn_fw2"]), (aw1[:, :], t["L3_gnn_aw1"]), (aw2[:, :], t["L3_gnn_aw2"]),
                    (ow1[:, :], t["L3_gnn_ow1"]), (ow2[:, :], t["L3_gnn_ow2"]),
                    (fb1[:, :], t["L3_gnn_fb1"].unsqueeze(1)), (ab1[:, :], t["L3_gnn_ab1"].unsqueeze(1)),
                    (ob1[:, :], t["L3_gnn_ob1"].unsqueeze(1)), (fb2[:, :], t["L3_gnn_fb2"].unsqueeze(0)),
                    (ab2[:, :], t["L3_gnn_ab2"].unsqueeze(0)), (ob2[:, :], t["L3_gnn_ob2"].unsqueeze(0)),
                ]
                for tile, name in ((keys[0], "dst"), (keys[1], "src"), (ew1, "edge_weight"), (ew2, "edge_weight_n2")):
                    loads.append((tile[:, 0:FULLC], t[name][0:P * FULLC].rearrange("(p c) -> p c", p=P)))
                    loads.append((tile[0:REST, FULLC:FULLC + 1], t[name][P * FULLC:E].unsqueeze(1)))

                @block.sync
                def _(sp):
                    sp.wait_ge(cleared, 8)
                    for to, of in loads:
                        sp.dma_start(to, of).then_inc(loaded, 16)

                @block.gpsimd
                def _(pool):
                    nc.gpsimd.iota(col_i[:, :], pattern=[[1, P]], base=0, channel_multiplier=0).then_inc(iotas, 1)
                    nc.gpsimd.iota(part_i[:, :], pattern=[[0, 1]], base=0, channel_multiplier=1).then_inc(iotas, 1)

                @block.vector
                def _(dve):
                    v = nc.vector
                    v.memset(X[:, NB - 1, :], 0.0).then_inc(cleared, 1)
                    v.memset(fw1[:, :], 0.0).then_inc(cleared, 1)
                    v.memset(keys[0][:, FULLC:NC], N).then_inc(cleared, 1)
                    v.memset(keys[1][:, FULLC:NC], N).then_inc(cleared, 1)
                    v.memset(ew1[:, FULLC:NC], 0.0).then_inc(cleared, 1)
                    v.memset(ew2[:, FULLC:NC], 0.0).then_inc(cleared, 1)
                    v.memset(zeros[:, :], 0.0).then_inc(cleared, 1)
                    v.memset(ones[:, :], 1.0).then_inc(cleared, 1)
                    for k in range(2):
                        v.memset(endi[k][:, NB:], 0)
                    for m in (src_d, dst_s, src_s):
                        v.memset(m[:, NC:NS], 0)
                    v.memset(meta_d[:, NC:NS, :], 0.0)
                    v.memset(meta_s[:, NC:NS, :], 0.0)
                    dve.wait_ge(iotas, 2)
                    v.tensor_copy(colf[:, :], col_i[:, :])
                    v.tensor_copy(iota[:, :], col_i[:, :])
                    v.tensor_copy(part[:, :], part_i[:, :])
                    v.drain()
                    v.tensor_scalar(ident[:, :], colf[:, :], part[:, 0:1], None, ALU.is_equal)
                    v.tensor_scalar(later[:, :], colf[:, :], part[:, 0:1], None, ALU.is_gt)
                    v.drain()
                    v.tensor_copy(identb[:, :], ident[:, :]).then_inc(consts, 1)
                    dve.wait_ge(loaded, 16 * len(loads))
                    v.tensor_scalar(wq[:, :], wq[:, :], HD ** -0.5, None, ALU.mult)
                    v.tensor_scalar(bq[:, :], bq[:, :], HD ** -0.5, None, ALU.mult)
                    inputs, hi, lo, scores = inkeys
                    v.tensor_copy(inputs[:, :, 0], keys[1][:, :])
                    v.tensor_copy(inputs[:, :, 1], ew1[:, :])
                    v.tensor_tensor(inputs[:, :, 2], ew1[:, :], ew2[:, :], ALU.mult)
                    v.tensor_copy(inputs[:, :, 3], keys[0][:, :])
                    v.tensor_copy(scores[:, :, 0], keys[0][:, :])
                    v.tensor_copy(scores[:, :, 1], keys[1][:, :])
                    for k in range(2):
                        v.drain()
                        v.tensor_scalar(cut[:, :], keys[k][:, :], 7, None, ALU.logical_shift_right)
                        v.drain()
                        v.tensor_copy(hi[k][:, :], cut[:, :])
                        v.drain()
                        v.tensor_scalar(cut[:, :], keys[k][:, :], P - 1, None, ALU.bitwise_and)
                        v.drain()
                        v.tensor_copy(lo[k][:, :], cut[:, :])
                    dve.wait_ge(wT, 1)
                    v.tensor_copy(w0[:, 0:D], psT[:, 0, :])
                    v.tensor_copy(w1[0][:, :], psT[:, 1, :])
                    v.tensor_copy(w1[1][:, :], psT[:, 2, :])
                    dve.wait_ge(a01, 1)
                    v.tensor_copy(w0[:, D:D + 2], psA[:, :])

                @block.tensor
                def _(pe):
                    pe.wait_ge(consts, 1)
                    pe.wait_ge(loaded, 16 * len(loads))
                    for k in range(3):
                        m = nc.tensor.transpose(psT[:, k, :], raw[:, k, :], ident[:, :])
                    m.then_inc(wT, 1)
                    nc.tensor.matmul(psA[:, :], raw[:, 0, :], acol[:, :], start=True, stop=True).then_inc(a01, 1)

        def attr_loads(sp, source, width, dst, free, unit, ready, rest):
            view = source[0:P * FULLC].rearrange("(p c) f -> p c f", p=P)

            def step(i, h):
                again(sp, free[h], i, unit)
                sp.dma_start(dst(h), view[:, bass.ds((i * 2 + h) * CH, CH), :]).then_inc(ready[h], 16)

            each(sp, CHUNKS - 1, 2, step)
            c0, h = NC - CH, (CHUNKS - 1) % 2
            again(sp, free[h], (CHUNKS - 1) // 2, unit)
            whole = FULLC - c0
            d = dst(h)
            sp.dma_start(d[0:REST, whole, :], source[P * FULLC:E]).then_inc(rest, 16)
            sp.dma_start(d[REST:P, whole, :], zeros[REST:P, 0:width]).then_inc(rest, 16)
            sp.dma_start(d[:, whole + 1, :], zeros[:, 0:width]).then_inc(rest, 16)
            sp.wait_ge(rest, 48)
            sp.dma_start(d[:, 0:whole, :], view[:, c0:FULLC, :]).then_inc(ready[h], 16)

        def count_edges(inkeys):
            inputs, hi, lo, scores = inkeys
            with semaphores(nc) as sem, ExitStack() as ctx:
                ea = ctx.enter_context(nc.sbuf_tensor("ea", [P, 2, CH, D], F32))
                eaT = ctx.enter_context(nc.sbuf_tensor("eaT", [P, 2, CH * P], F32))
                B = ctx.enter_context(nc.sbuf_tensor("Bc", [P, 2, 2, CH, P], BF16))
                A = ctx.enter_context(nc.sbuf_tensor("Ac", [P, 2, 2, CH, NB], BF16))
                zb = ctx.enter_context(nc.sbuf_tensor("zb", [P, P], BF16))
                sums = ctx.enter_context(nc.sbuf_tensor("sums", [P, 2, NB], F32))
                psE = [ctx.enter_context(nc.psum_tensor(f"psE{h}", [P, CH * P], F32)) for h in range(2)]
                psS = [ctx.enter_context(nc.psum_tensor(f"psS{h}", [P, CH, NH], F32)) for h in range(2)]
                psC = [ctx.enter_context(nc.psum_tensor(f"psC{k}", [P, 512], F32)) for k in range(2)]
                s = {n: sem(n) for n in (
                    "ea_ready0", "ea_ready1", "ea_free0", "ea_free1", "ea_rest", "hot", "counted", "flipped",
                    "eaT_ready", "scored", "score_kept", "zb_ready", "all_counted", "between", "total")}
                block = ctx.enter_context(nc.Block())

                @block.sync
                def _(sp):
                    attr_loads(sp, t["edge_attr_128"], D, lambda h: ea[:, h], [s["ea_free0"], s["ea_free1"]], 16,
                               [s["ea_ready0"], s["ea_ready1"]], s["ea_rest"])

                @block.vector
                def _(dve):
                    v = nc.vector
                    v.memset(zb[:, :], 0.0).then_inc(s["zb_ready"], 1)

                    def hot(i, h):
                        k0 = i * 2 + h
                        if not (isinstance(k0, int) and k0 < 2):
                            dve.wait_ge(s["counted"], k0 - 1)
                        for k in range(2):
                            v.tensor_tensor(A[:, h, k], over(iota[:, 0:NB], CH),
                                            along(hi[k][:, bass.ds(k0 * CH, CH)], NB), ALU.is_equal)
                            m = v.tensor_tensor(B[:, h, k], over(iota[:, :], CH),
                                                along(lo[k][:, bass.ds(k0 * CH, CH)], P), ALU.is_equal)
                        m.then_inc(s["hot"], 1)

                    def score(i, h):
                        k0 = i * 2 + h
                        dve.wait_ge(s["scored"], k0 + 1)
                        v.tensor_tensor(scores[:, bass.ds(k0 * CH, CH), 2:2 + NH], psS[h][:, :, :],
                                        over(be[:, :], CH), ALU.add).then_inc(s["score_kept"], 1)

                    def step(i, h):
                        hot(i + (h + 1) // 2, (h + 1) % 2)
                        score(i, h)

                    hot(0, 0)
                    each(dve, CHUNKS - 1, 2, step)
                    score((CHUNKS - 1) // 2, (CHUNKS - 1) % 2)
                    dve.wait_ge(s["all_counted"], 1)
                    for k in range(2):
                        v.tensor_copy(count[k][:, :], psC[k][:, 0:NB])
                    v.drain()
                    for k in range(2):
                        v.tensor_scalar(has[k][:, :], count[k][:, :], 1.0, None, ALU.min)
                    v.memset(sums[:, :, :], 0.0).then_inc(s["total"], 1)
                    dve.wait_ge(s["between"], 1)
                    for k in range(2):
                        v.tensor_tensor_scan(sums[:, k, 1:NB], ones[:, 0:NB - 1], psE[0][:, k * P:k * P + NB - 1],
                                             0.0, ALU.mult, ALU.add)
                    v.drain()
                    for k in range(2):
                        v.tensor_tensor(base[k][:, :], sums[:, k, :], psE[1][:, k * P:k * P + NB], ALU.add)

                @block.scalar
                def _(act):
                    def step(i, h):
                        act.wait_ge(s["flipped"], i * 2 + h + 1)
                        nc.scalar.copy(eaT[:, h, :], psE[h][:, :]).then_inc(s["eaT_ready"], 1)
                        act.sem_inc(s[f"ea_free{h}"], 16)

                    each(act, CHUNKS, 2, step)

                @block.tensor
                def _(pe):
                    pe.wait_ge(s["zb_ready"], 1)
                    for k in range(2):
                        nc.tensor.matmul(psC[k][:, 0:NB], zb[:, :], zb[:, 0:NB], start=True, stop=False)

                    def flip(i, h):
                        if not (isinstance(i, int) and i * 2 + h < 2):
                            pe.wait_ge(s["eaT_ready"], i * 2 + h - 1)
                        pe.wait_ge(s[f"ea_ready{h}"], 16 * (i + 1))
                        for j in range(CH):
                            m = nc.tensor.transpose(psE[h][:, j * P:(j + 1) * P], ea[:, h, j, :], ident[:, :])
                        m.then_inc(s["flipped"], 1)

                    def step(i, h, last=False):
                        k0 = i * 2 + h
                        if not last:
                            flip(i + (h + 1) // 2, (h + 1) % 2)
                        pe.wait_ge(s["hot"], k0 + 1)
                        for j in range(CH):
                            for k in range(2):
                                m = nc.tensor.matmul(psC[k][:, 0:NB], B[:, h, k, j, :], A[:, h, k, j, :],
                                                     start=False, stop=False)
                        m.then_inc(s["counted"], 1)
                        if not (isinstance(k0, int) and k0 < 2):
                            pe.wait_ge(s["score_kept"], k0 - 1)
                        pe.wait_ge(s["eaT_ready"], k0 + 1)
                        for j in range(CH):
                            m = nc.tensor.matmul(psS[h][:, j, :], eaT[:, h, j * P:(j + 1) * P], we[:, :],
                                                 start=True, stop=True)
                        m.then_inc(s["scored"], 1)

                    flip(0, 0)
                    each(pe, CHUNKS - 1, 2, step)
                    step((CHUNKS - 1) // 2, (CHUNKS - 1) % 2, last=True)
                    for k in range(2):
                        m = nc.tensor.matmul(psC[k][:, 0:NB], zb[:, :], zb[:, 0:NB], start=False, stop=True)
                    m.then_inc(s["all_counted"], 1)
                    pe.wait_ge(s["total"], 1)
                    for k in range(2):
                        nc.tensor.matmul(psE[0][:, k * P:k * P + NB], ones[:, :], count[k][:, :], start=True, stop=True)
                        m = nc.tensor.matmul(psE[1][:, k * P:k * P + NB], later[:, :], count[k][:, :],
                                             start=True, stop=True)
                    m.then_inc(s["between"], 1)

        def sort_edges(inkeys):
            inputs, hi, lo, scores = inkeys
            with semaphores(nc) as sem, ExitStack() as ctx:
                B = ctx.enter_context(nc.sbuf_tensor("Bs", [P, 2, 2, CH, P], BF16))
                A = ctx.enter_context(nc.sbuf_tensor("As", [P, 2, 2, CH, NB], BF16))
                BT = [ctx.enter_context(nc.sbuf_tensor(f"BT{k}", [P, CH * P], F32)) for k in range(2)]
                M = [ctx.enter_context(nc.sbuf_tensor(f"M{k}", [P, CH, P], BF16)) for k in range(2)]
                run = [ctx.enter_context(nc.sbuf_tensor(f"run{k}", [P, CH, NB], F32)) for k in range(2)]
                hit = ctx.enter_context(nc.sbuf_tensor("hit", [P, 2, CH, NB], F32))
                posf = ctx.enter_context(nc.sbuf_tensor("posf", [P, 2, CH], F32))
                pos = ctx.enter_context(nc.sbuf_tensor("pos", [P, 2, 2, CH], I32))
                rec_d = ctx.enter_context(nc.sbuf_tensor("rec_d", [P, 2, CH, PW], F32))
                rec_s = ctx.enter_context(nc.sbuf_tensor("rec_s", [P, 2, CH, SW], F32))
                psB = [ctx.enter_context(nc.psum_tensor(f"psB{k}", [P, CH * P], BF16)) for k in range(2)]
                psG = [ctx.enter_context(nc.psum_tensor(f"psG{k}", [P, 512], F32)) for k in range(2)]
                psR = [ctx.enter_context(nc.psum_tensor(f"psR{k}", [P, 512], F32)) for k in range(2)]
                psQ = ctx.enter_context(nc.psum_tensor("psQ", [P, CH, P], F32))

                def gaps(ps):
                    return ps[:, 0:CH * NB].rearrange("p (j b) -> p j b", j=CH)

                s = {n: sem("so_" + n) for n in (
                    "hot", "eq", "masked", "rest", "cleared", "rec_s_ready", "go", "at_ready0", "at_ready1",
                    "flip0", "flip1", "BT_ready0", "BT_ready1", "added0", "added1", "run0", "run1",
                    "ranked0", "ranked1", "placed0", "placed1", "in_d_ready",
                    "sent_d0", "sent_d1", "sent_s0", "sent_s1")}
                sent = [[s["sent_d0"], s["sent_d1"]], [s["sent_s0"], s["sent_s1"]]]
                block = ctx.enter_context(nc.Block())

                @block.sync
                def _(sp):
                    sp.wait_ge(s["cleared"], 1)
                    attr_loads(sp, t["edge_attr_50"], NG, lambda h: rec_d[:, h, :, 4:4 + NG],
                               sent[0], 16 * CH, [s["at_ready0"], s["at_ready1"]], s["rest"])

                @block.gpsimd
                def _(pool):
                    def step(i, h):
                        for k, (rec, table) in enumerate(((rec_d, sorted_d), (rec_s, sorted_s))):
                            pool.wait_ge(s[f"placed{k}"], i * 2 + h + 2)
                            if k == 0:
                                pool.wait_ge(s[f"at_ready{h}"], 16 * (i + 1))
                                pool.wait_ge(s["in_d_ready"], i * 2 + h + 1)
                            else:
                                pool.wait_ge(s["rec_s_ready"], i * 2 + h + 1)
                            pool.sem_inc(s["go"], 1)
                            for j in range(CH):
                                nc.gpsimd.indirect_dma_start(
                                    out=table[:, :], out_offset=bass.IndirectOffsetOnAxis(ap=pos[:, k, h, j:j + 1], axis=0),
                                    in_=rec[:, h, j, :], in_offset=None).then_inc(sent[k][h], 16)

                    each(pool, CHUNKS, 2, step)
                    for k in range(2):
                        for h in range(2):
                            pool.wait_ge(sent[k][h], 16 * CH * (CHUNKS // 2))

                @block.vector
                def _(dve):
                    v = nc.vector
                    v.memset(rec_d[:, :, :, :], 0.0)
                    v.memset(rec_s[:, :, :, :], 0.0).then_inc(s["cleared"], 1)
                    dve.sem_inc(s["masked"], 1)
                    for k in range(2):
                        dve.sem_inc(s[f"placed{k}"], 1)

                    def hot(i, h):
                        k0 = i * 2 + h
                        for k in range(2):
                            v.tensor_tensor(A[:, h, k], over(iota[:, 0:NB], CH),
                                            along(hi[k][:, bass.ds(k0 * CH, CH)], NB), ALU.is_equal)
                            m = v.tensor_tensor(B[:, h, k], over(iota[:, :], CH),
                                                along(lo[k][:, bass.ds(k0 * CH, CH)], P), ALU.is_equal)
                        m.then_inc(s["hot"], 1)

                    def rank(i, h):
                        k0 = i * 2 + h
                        for k in range(2):
                            dve.wait_ge(s["eq"], 2 * k0 + k + 1)
                            dve.wait_ge(s[f"ranked{k}"], k0 + 1)
                            v.tensor_tensor(M[k][:, :, :], psQ[:, :, :], over(later[:, :], CH),
                                            ALU.mult).then_inc(s["masked"], 1)

                    def place(i, h):
                        k0 = i * 2 + h
                        for k in range(2):
                            dve.wait_ge(s[f"ranked{k}"], k0 + 2)
                            v.tensor_tensor(hit[:, k], gaps(psG[k]), A[:, h, k], ALU.mult)
                        v.drain()
                        for k in range(2):
                            v.tensor_reduce(posf[:, k, :], hit[:, k], AX.X, ALU.add)
                        v.drain()
                        for k in range(2):
                            again(dve, sent[k][h], i, 16 * CH)
                            v.tensor_copy(pos[:, k, h, :], posf[:, k, :]).then_inc(s[f"placed{k}"], 1)

                    hot(0, 0)

                    def step(i, h, last=False):
                        rank(i, h)
                        if not last:
                            hot(i + (h + 1) // 2, (h + 1) % 2)
                        place(i, h)

                    each(dve, CHUNKS - 1, 2, step)
                    step((CHUNKS - 1) // 2, (CHUNKS - 1) % 2, last=True)

                @block.scalar
                def _(act):
                    for k in range(2):
                        act.sem_inc(s[f"BT_ready{k}"], 1)
                        act.wait_ge(s[f"added{k}"], 1)
                        nc.scalar.copy(run[k][:, 0, :], psR[k][:, 0:NB]).then_inc(s[f"run{k}"], 1)
                    act.wait_ge(s["cleared"], 1)

                    def step(i, h):
                        k0 = i * 2 + h
                        for k in range(2):
                            act.wait_ge(s[f"flip{k}"], k0 + 1)
                            act.wait_ge(s[f"ranked{k}"], k0 + 1)
                            nc.scalar.copy(BT[k][:, :], psB[k][:, :]).then_inc(s[f"BT_ready{k}"], 1)
                        again(act, sent[0][h], i, 16 * CH)
                        nc.scalar.copy(rec_d[:, h, :, 0:4], inputs[:, bass.ds(k0 * CH, CH), :]).then_inc(s["in_d_ready"], 1)
                        again(act, sent[1][h], i, 16 * CH)
                        nc.scalar.copy(rec_s[:, h, :, 0:2 + NH], scores[:, bass.ds(k0 * CH, CH), :]).then_inc(
                            s["rec_s_ready"], 1)
                        for j in range(CH):
                            for k in range(2):
                                act.wait_ge(s[f"added{k}"], k0 * CH + j + 2)
                                nc.scalar.copy(run[k][:, (j + 1) % CH, :], psR[k][:, 0:NB]).then_inc(s[f"run{k}"], 1)

                    each(act, CHUNKS, 2, step)

                @block.tensor
                def _(pe):
                    for k in range(2):
                        pe.sem_inc(s[f"ranked{k}"], 1)
                        nc.tensor.matmul(psR[k][:, 0:NB], ident[:, :], base[k][:, :], start=True,
                                         stop=True).then_inc(s[f"added{k}"], 1)

                    def step(i, h):
                        k0 = i * 2 + h
                        pe.wait_ge(s["hot"], k0 + 1)
                        for k in range(2):
                            pe.wait_ge(s[f"BT_ready{k}"], k0 + 1)
                            for j in range(CH):
                                m = nc.tensor.transpose(psB[k][:, j * P:(j + 1) * P], B[:, h, k, j, :], identb[:, :])
                            m.then_inc(s[f"flip{k}"], 1)
                        for k in range(2):
                            pe.wait_ge(s[f"BT_ready{k}"], k0 + 2)
                            pe.wait_ge(s["masked"], 2 * k0 + k + 1)
                            for j in range(CH):
                                b = BT[k][:, j * P:(j + 1) * P]
                                m = nc.tensor.matmul(psQ[:, j, :], b, b, start=True, stop=True)
                            m.then_inc(s["eq"], 1)
                        for k in range(2):
                            pe.wait_ge(s["masked"], 2 * k0 + k + 2)
                            pe.wait_ge(s[f"placed{k}"], k0 + 1)
                        for j in range(CH):
                            for k in range(2):
                                pe.wait_ge(s[f"run{k}"], k0 * CH + j + 1)
                                nc.tensor.matmul(gaps(psG[k])[:, j, :], BT[k][:, j * P:(j + 1) * P], run[k][:, j, :],
                                                 start=True, stop=False)
                                m = nc.tensor.matmul(gaps(psG[k])[:, j, :], M[k][:, j, :], A[:, h, k, j, :],
                                                     start=False, stop=True)
                                if j == CH - 1:
                                    m.then_inc(s[f"ranked{k}"], 1)
                                nc.tensor.matmul(psR[k][:, 0:NB], B[:, h, k, j, :], A[:, h, k, j, :], start=False,
                                                 stop=True, skip_group_check=True).then_inc(s[f"added{k}"], 1)

                    each(pe, CHUNKS, 2, step)

        def order_edges():
            with semaphores(nc) as sem, ExitStack() as ctx:
                GC = NC // 8
                rd = ctx.enter_context(nc.sbuf_tensor("rd", [P, GC, PW], F32))
                rs = ctx.enter_context(nc.sbuf_tensor("rs", [P, GC, SW], F32))
                key = [ctx.enter_context(nc.sbuf_tensor(f"key{k}", [P, NC], F32)) for k in range(2)]
                alike = ctx.enter_context(nc.sbuf_tensor("alike", [P, NC], F32))
                run = ctx.enter_context(nc.sbuf_tensor("run", [P, 1], F32))
                flag = ctx.enter_context(nc.sbuf_tensor("flag", [P, 4], F32))
                last = ctx.enter_context(nc.sbuf_tensor("last", [P, NB], F32))
                past = ctx.enter_context(nc.sbuf_tensor("past", [P, 1], F32))
                psK = [ctx.enter_context(nc.psum_tensor(f"psK{k}", [P, P], F32)) for k in range(4)]
                s = {n: sem("or_" + n) for n in (
                    "landed", "taken", "keys", "firsts", "goes", "turned")}
                block = ctx.enter_context(nc.Block())

                @block.sync
                def _(sp):
                    for g in range(8):
                        if g:
                            sp.wait_ge(s["taken"], g)
                        sp.dma_start(rd[:, :, :], sorted_d.rearrange("(p c) w -> p c w", p=P)[
                            :, g * GC:(g + 1) * GC, :]).then_inc(s["landed"], 16)
                        sp.dma_start(rs[:, :, :], sorted_s.rearrange("(p c) w -> p c w", p=P)[
                            :, g * GC:(g + 1) * GC, :]).then_inc(s["landed"], 16)

                @block.vector
                def _(dve):
                    v = nc.vector
                    for g in range(8):
                        dve.wait_ge(s["landed"], 32 * (g + 1))
                        cs = slice(g * GC, (g + 1) * GC)
                        v.tensor_copy(src_d[:, cs], rd[:, :, 0])
                        v.tensor_copy(meta_d[:, cs, 2], rd[:, :, 1])
                        v.tensor_copy(meta_d[:, cs, 4], rd[:, :, 2])
                        v.tensor_copy(key[0][:, cs], rd[:, :, 3])
                        v.tensor_copy(dst_s[:, cs], rs[:, :, 0])
                        v.tensor_copy(src_s[:, cs], rs[:, :, 1])
                        v.tensor_copy(key[1][:, cs], rs[:, :, 1])
                        v.tensor_copy(meta_s[:, cs, 2:2 + NH], rs[:, :, 2:2 + NH]).then_inc(s["taken"], 1)
                    v.drain().then_inc(s["keys"], 1)
                    for k, meta in ((0, meta_d), (1, meta_s)):
                        v.memset(meta[:, 0:1, 0], 0.0)
                        v.tensor_tensor(meta[:, 1:NC, 0], key[k][:, 1:NC], key[k][:, 0:NC - 1], ALU.is_equal)
                        v.drain()
                        v.tensor_scalar(meta[:, 0:NC, 1], meta[:, 0:NC, 0], 1.0, BIG, ALU.subtract, ALU.mult)
                        v.tensor_tensor(last[:, :], base[k][:, :], count[k][:, :], ALU.add)
                        v.drain()
                        v.tensor_scalar(last[:, :], last[:, :], -1.0, None, ALU.add)
                        v.drain()
                        v.tensor_scalar(endi[k][:, 0:NB], last[:, :], 0.0, None, ALU.max)
                    dve.wait_ge(s["firsts"], 1)
                    for k in range(2):
                        v.scalar_tensor_tensor(out=goes[k][:, :], in0=psK[k][:, :], scalar=key[k][:, NC - 1:NC],
                                               in1=later[:, :], op0=ALU.is_equal, op1=ALU.mult)
                    v.drain().then_inc(s["goes"], 1)
                    dve.wait_ge(s["turned"], 1)
                    for k in range(2):
                        v.tensor_copy(goesT[k][:, :], psK[2 + k][:, :])
                        v.tensor_scalar(shut[k][:, :], psK[2 + k][:, :], 1.0, BIG, ALU.subtract, ALU.mult)
                    v.tensor_copy(firsti[:, :], key[0][:, 0:1])
                    v.tensor_scalar(past[:, :], part[:, :], float(EP), None, ALU.add)
                    v.drain()
                    for k in range(2):
                        v.tensor_scalar(alike[:, :], key[k][:, :], key[k][:, 0:1], None, ALU.is_equal)
                        v.tensor_reduce(flag[:, 0:1], goesT[k][:, :], AX.X, ALU.max)
                        v.tensor_reduce(flag[:, 1:2], goes[k][:, :], AX.X, ALU.max)
                        v.drain()
                        v.tensor_reduce(run[:, :], alike[:, :], AX.X, ALU.add)
                        v.drain()
                        v.tensor_scalar(flag[:, 2:3], run[:, :], float(NC), None, ALU.is_ge)
                        v.drain()
                        v.tensor_tensor(flag[:, 2:3], flag[:, 2:3], flag[:, 1:2], ALU.mult)
                        v.drain()
                        v.tensor_tensor(flag[:, 0:1], flag[:, 0:1], flag[:, 2:3], ALU.is_gt)
                        v.scalar_tensor_tensor(out=flag[:, 3:4], in0=part[:, :], scalar=float(NC - 1), in1=run[:, :],
                                               op0=ALU.mult, op1=ALU.add)
                        v.drain()
                        v.tensor_scalar(flag[:, 3:4], flag[:, 3:4], float(-1 - EP), None, ALU.add)
                        v.drain()
                        v.tensor_tensor(flag[:, 3:4], flag[:, 3:4], flag[:, 0:1], ALU.mult)
                        v.drain()
                        v.tensor_tensor(carryi[k][:, :], flag[:, 3:4], past[:, :], ALU.add)
                    v.tensor_scalar(last[:, :], base[0][:, :], past[:, :], None, ALU.subtract)
                    v.drain()
                    v.tensor_tensor(last[:, :], last[:, :], has[0][:, :], ALU.mult)
                    v.drain()
                    v.tensor_scalar(starti[:, :], last[:, :], past[:, :], None, ALU.add)

                @block.tensor
                def _(pe):
                    pe.wait_ge(s["keys"], 1)
                    for k in range(2):
                        m = nc.tensor.matmul(psK[k][:, :], key[k][:, 0:1].to_broadcast([P, P]), ident[:, :],
                                             start=True, stop=True)
                    m.then_inc(s["firsts"], 1)
                    pe.wait_ge(s["goes"], 1)
                    for k in range(2):
                        m = nc.tensor.transpose(psK[2 + k][:, :], goes[k][:, :], ident[:, :])
                    m.then_inc(s["turned"], 1)

        def spread_ad():
            with semaphores(nc) as sem, ExitStack() as ctx:
                sown = ctx.enter_context(nc.sbuf_tensor("sown", [P, NC], F32))
                filled = ctx.enter_context(nc.sbuf_tensor("filled", [P, NC], F32))
                same = ctx.enter_context(nc.sbuf_tensor("same", [P, NC], F32))
                first = ctx.enter_context(nc.sbuf_tensor("first", [P, 1], F32))
                s = {n: sem("ad_" + n) for n in ("zeroed", "written", "sown", "first",
                                                                            "back", "clear")}
                block = ctx.enter_context(nc.Block())

                @block.vector
                def _(dve):
                    v = nc.vector
                    v.memset(filled[:, :], 0.0).then_inc(s["clear"], 1)
                    v.tensor_copy(same[:, :], meta_d[:, 0:NC, 0])
                    dve.wait_ge(s["back"], 16)
                    dve.wait_ge(s["first"], 16)
                    dve.wait_ge(s["zeroed"], 16)
                    v.tensor_copy(sown[:, 0:1], first[:, :])
                    v.drain()
                    v.tensor_tensor_scan(filled[:, :], same[:, :], sown[:, :], 0.0, ALU.mult, ALU.add)
                    v.drain()
                    v.tensor_copy(meta_d[:, 0:NC, 3], filled[:, :])

                @block.sync
                def _(sp):
                    sp.wait_ge(s["clear"], 1)
                    sp.dma_start(ADE[0:EP].rearrange("(p c) w -> p (c w)", p=P), filled[:, :]).then_inc(s["zeroed"], 16)
                    with nc.allow_non_contiguous_dma(reason="a column of a node table"):
                        sp.dma_start(ADT.rearrange("(b p) w -> p (b w)", p=P), AD[:, :]).then_inc(s["written"], 16)
                    sp.wait_ge(s["sown"], 16 * NB)
                    sp.dma_start(sown[:, :], ADE[0:EP].rearrange("(p c) w -> p (c w)", p=P)).then_inc(s["back"], 16)

                @block.gpsimd
                def _(pool):
                    pool.wait_ge(s["zeroed"], 16)
                    for b in range(NB):
                        nc.gpsimd.indirect_dma_start(
                            out=ADE[:, :], out_offset=bass.IndirectOffsetOnAxis(ap=starti[:, b:b + 1], axis=0),
                            in_=AD[:, b:b + 1], in_offset=None).then_inc(s["sown"], 16)
                    pool.wait_ge(s["written"], 16)
                    nc.gpsimd.indirect_dma_start(
                        out=first[:, :], out_offset=None, in_=ADT[:, :],
                        in_offset=bass.IndirectOffsetOnAxis(ap=firsti[:, 0:1], axis=0)).then_inc(s["first"], 16)

        def edge_pass(layer, tag, table, states):
            soft = layer in (0, 2)
            k = 1 if layer == 2 else 0
            meta = (meta_d, meta_s)[k]
            nf = meta[:, 0:1, :].shape[2]
            width = {0: W0, 1: D, 2: W2, 3: D}[layer]
            used = {0: D + 1, 1: D, 2: NH * (HD + 1), 3: D}[layer]
            heads = NH if layer == 2 else 1
            gathers = [(table, KVW if layer == 2 else table.shape[1], dst_s if layer == 2 else src_d)]
            if layer == 2:
                gathers.append((TQ, D, src_s))
            with semaphores(nc) as sem, ExitStack() as ctx:
                def sb(n, shape, dt=F32):
                    return ctx.enter_context(nc.sbuf_tensor(f"{tag}_{n}", shape, dt))

                got_rows = [sb(f"rows{m}", [P, SLOTS, CH, w]) for m, (_, w, _) in enumerate(gathers)]
                G = got_rows[0]
                ix = sb("ix", [P, len(gathers), SLOTS, CH], I32)
                mb = sb("mb", [P, SLOTS, CH, nf])
                O = sb("O", [P, SLOTS, CH, width])
                top_ = sb("top", [P, SLOTS, CH + 1, heads])
                sc = sb("sc", [P, SLOTS, 3, CH, heads])
                coef = sb("coef", [P, SLOTS, 2, CH, heads])
                if layer == 2:
                    prod = sb("prod", [P, CH, D])
                if layer == 3:
                    at = sb("at", [P, SLOTS, CH, PW])
                    aT = sb("aT", [P, CH // 2 * P])
                    hT = sb("hT", [P, CH * P])
                    psT = ctx.enter_context(nc.psum_tensor(f"{tag}_psT", [P, CH // 2 * P], F32))
                    psH = ctx.enter_context(nc.psum_tensor(f"{tag}_psH", [P, CH * P], F32))
                    psW = [ctx.enter_context(nc.psum_tensor(f"{tag}_psW{h}", [P, CH, P], F32)) for h in range(2)]
                s = {n: sem(f"{tag}_{n}") for n in (
                    "fields", "go", "done", "clear", "diffs", "coefs", "messages", "at_turned", "aT", "hidden",
                    "hT", "filters")}
                got = [sem(f"{tag}_got{h}") for h in range(SLOTS)]
                stored = [sem(f"{tag}_stored{h}") for h in range(SLOTS)]
                at_here = [sem(f"{tag}_at{h}") for h in range(SLOTS)]
                unit = 16 * CH * len(gathers)
                block = ctx.enter_context(nc.Block())

                def since(eng, sem, i, h, back):
                    if not (isinstance(i, int) and i * SLOTS + h < back):
                        eng.wait_ge(sem, i * SLOTS + h + 1 - back)

                @block.gpsimd
                def _(pool):
                    def step(i, h):
                        since(pool, s["done"], i, h, SLOTS)
                        pool.wait_ge(s["fields"], i * SLOTS + h + 1)
                        pool.sem_inc(s["go"], 1)
                        for j in range(CH):
                            for m, (tab, w, _) in enumerate(gathers):
                                nc.gpsimd.indirect_dma_start(
                                    out=got_rows[m][:, h, j, :], out_offset=None, in_=tab[:, :],
                                    in_offset=bass.IndirectOffsetOnAxis(ap=ix[:, m, h, j:j + 1], axis=0)
                                ).then_inc(got[h], 16)

                    each(pool, CHUNKS, SLOTS, step)

                @block.sync
                def _(sp):
                    sview = states[0:EP].rearrange("(p c) w -> p c w", p=P)
                    dview = sorted_d.rearrange("(p c) w -> p c w", p=P)

                    def load(i, h):
                        since(sp, s["at_turned"], i, h, SLOTS)
                        sp.dma_start(at[:, h, :, :], dview[:, bass.ds((i * SLOTS + h) * CH, CH), :]).then_inc(
                            at_here[h], 16)

                    def step(i, h, ahead=True):
                        if layer == 3 and ahead:
                            load(i + (h + 2) // SLOTS, (h + 2) % SLOTS)
                        sp.wait_ge(s["done"], i * SLOTS + h + 1)
                        sp.dma_start(sview[:, bass.ds((i * SLOTS + h) * CH, CH), :], O[:, h, :, :]).then_inc(
                            stored[h], 16)

                    if layer == 3:
                        load(0, 0)
                        load(0, 1)
                    each(sp, CHUNKS - 2, SLOTS, step)
                    for c in range(CHUNKS - 2, CHUNKS):
                        step(c // SLOTS, c % SLOTS, ahead=False)
                    for h in range(SLOTS):
                        sp.wait_ge(stored[h], 16 * (CHUNKS // SLOTS))

                @block.scalar
                def _(act):
                    def fetch(i, h, c0):
                        again(act, got[h], i, unit)
                        since(act, s["done"], i, h, SLOTS)
                        for m, (_, _, idx) in enumerate(gathers):
                            nc.scalar.copy(ix[:, m, h, :], idx[:, bass.ds(c0, CH)])
                        nc.scalar.copy(mb[:, h, :, :], meta[:, bass.ds(c0, CH), :]).then_inc(s["fields"], 1)

                    fetch(0, 0, 0)
                    fetch(0, 1, CH)

                    def step(i, h):
                        k0 = i * SLOTS + h
                        act.wait_ge(got[h], (i + 1) * unit)
                        fetch(i + (h + 2) // SLOTS, (h + 2) % SLOTS, (k0 + 2) * CH)
                        if layer == 3:
                            act.wait_ge(s["at_turned"], k0 + 1)
                            nc.scalar.copy(aT[:, :], psT[:, :]).then_inc(s["aT"], 1)
                            act.wait_ge(s["hidden"], k0 + 1)
                            nc.scalar.activation(hT[:, :], psH[:, :], ACT.Silu, bias=fb1[:, 0:1]).then_inc(s["hT"], 1)
                        if layer == 1:
                            act.wait_ge(s["fields"], k0 + 1)
                            for j in range(CH):
                                m = nc.scalar.activation(G[:, h, j, :], G[:, h, j, :], ACT.Copy,
                                                         scale=mb[:, h, j, 4:5])
                            m.then_inc(s["messages"], 1)
                        if soft:
                            act.wait_ge(s["diffs"], k0 + 1)
                            nc.scalar.activation(coef[:, h], sc[:, h, 1:3], ACT.Exp).then_inc(s["coefs"], 1)
                        if layer == 0:
                            act.wait_ge(s["coefs"], k0 + 1)
                            for j in range(CH):
                                m = nc.scalar.activation(G[:, h, j, 0:used], G[:, h, j, 0:used], ACT.Copy,
                                                         scale=coef[:, h, 1, j, :])
                            m.then_inc(s["messages"], 1)

                    each(act, CHUNKS, SLOTS, step)

                @block.vector
                def _(dve):
                    v = nc.vector
                    v.memset(O[:, :, :, :], 0.0)
                    v.memset(top_[:, :, :, :], 0.0)
                    v.drain()

                    def scores_(i, h):
                        k0, hp = i * SLOTS + h, (h - 1) % SLOTS
                        dve.wait_ge(got[h], (i + 1) * unit)
                        dve.wait_ge(s["fields"], k0 + 1)
                        v.tensor_copy(top_[:, h, 0, :], top_[:, hp, CH, :])
                        if layer == 0:
                            a, b = sc[:, h, 0, :, 0], top_[:, h, 1:CH + 1, 0]
                            v.tensor_tensor(a, G[:, h, :, D + 1], mb[:, h, :, 3], ALU.add)
                            v.drain()
                            v.scalar_tensor_tensor(out=a, in0=a, scalar=0.2, in1=a, op0=ALU.mult, op1=ALU.max)
                            v.drain()
                            v.tensor_tensor(a, a, mb[:, h, :, 2], ALU.mult)
                            v.drain()
                            v.tensor_tensor_scan(b, mb[:, h, :, 0], a, top_[:, h, 0, :], ALU.mult, ALU.max)
                            v.drain()
                        else:
                            Q = got_rows[1]
                            v.tensor_tensor(prod[:, :, :], G[:, h, :, 0:D], Q[:, h, :, :], ALU.mult)
                            v.drain()
                            v.tensor_reduce(sc[:, h, 0, :, :], prod[:, :, :].rearrange("p c (h d) -> p c h d", h=NH),
                                            AX.X, ALU.add)
                            v.drain()
                            v.tensor_tensor(sc[:, h, 0, :, :], sc[:, h, 0, :, :], mb[:, h, :, 2:2 + NH], ALU.add)
                            v.drain()
                            for j in range(CH):
                                v.scalar_tensor_tensor(out=top_[:, h, j + 1, :], in0=top_[:, h, j, :],
                                                       scalar=mb[:, h, j, 1:2], in1=sc[:, h, 0, j, :],
                                                       op0=ALU.add, op1=ALU.max)
                                v.drain()
                        v.tensor_tensor(sc[:, h, 1], top_[:, h, 0:CH, :], along(mb[:, h, :, 1], heads), ALU.add)
                        v.tensor_tensor(sc[:, h, 2], sc[:, h, 0], top_[:, h, 1:CH + 1, :], ALU.subtract)
                        v.drain()
                        v.tensor_tensor(sc[:, h, 1], sc[:, h, 1], top_[:, h, 1:CH + 1, :],
                                        ALU.subtract).then_inc(s["diffs"], 1)

                    def sums(i, h):
                        k0, hp = i * SLOTS + h, (h - 1) % SLOTS
                        if layer in (0, 1):
                            dve.wait_ge(s["messages"], k0 + 1)
                        dve.wait_ge(s["fields"], k0 + 1)
                        if layer == 3:
                            dve.wait_ge(got[h], (i + 1) * unit)
                            dve.wait_ge(s["filters"], k0 + 1)
                            v.tensor_tensor(G[:, h], psW[h % 2][:, :, :], G[:, h], ALU.mult)
                        if layer == 2:
                            dve.wait_ge(s["coefs"], k0 + 1)
                            V = G[:, h, :, D:KVW].rearrange("p c (h d) -> p c h d", h=NH)
                            v.tensor_tensor(V, V, coef[:, h, 1].unsqueeze(3).to_broadcast([P, CH, NH, HD + 1]), ALU.mult)
                        if layer in (2, 3):
                            v.drain()
                        again(dve, stored[h], i, 16)
                        if layer in (0, 2):
                            at0 = D + 2 if layer == 0 else used
                            v.tensor_copy(O[:, h, :, at0:at0 + heads], top_[:, h, 1:CH + 1, :])
                        off = D if layer == 2 else 0
                        for j in range(CH):
                            before = O[:, hp, CH - 1, 0:used] if j == 0 else O[:, h, j - 1, 0:used]
                            now = O[:, h, j, 0:used]
                            if layer == 2:
                                v.tensor_tensor(now.rearrange("p (h d) -> p h d", h=NH),
                                                before.rearrange("p (h d) -> p h d", h=NH),
                                                along(coef[:, h, 0, j, :], HD + 1), ALU.mult)
                                v.drain()
                                m = v.tensor_tensor(now, now, G[:, h, j, off:off + used], ALU.add)
                            else:
                                f = coef[:, h, 0, j, :] if layer == 0 else mb[:, h, j, 0:1]
                                m = v.scalar_tensor_tensor(out=now, in0=before, scalar=f, in1=G[:, h, j, 0:used],
                                                           op0=ALU.mult, op1=ALU.add)
                            if j < CH - 1:
                                v.drain()
                        m.then_inc(s["done"], 1)
                        v.drain()

                    if not soft:
                        each(dve, CHUNKS, SLOTS, sums)
                    else:
                        scores_(0, 0)

                        def step(i, h):
                            scores_(i + (h + 1) // SLOTS, (h + 1) % SLOTS)
                            sums(i, h)

                        each(dve, CHUNKS - 1, SLOTS, step)
                        sums((CHUNKS - 1) // SLOTS, (CHUNKS - 1) % SLOTS)
                    v.tensor_copy(ends[:, 0:width], O[:, (CHUNKS - 1) % SLOTS, CH - 1, :])

                if layer == 3:
                    @block.tensor
                    def _(pe):
                        def step(i, h):
                            k0 = i * SLOTS + h
                            since(pe, s["aT"], i, h, 1)
                            pe.wait_ge(at_here[h], (i + 1) * 16)
                            for q in range(CH // 2):
                                m = nc.tensor.transpose(
                                    psT[:, q * P:(q + 1) * P],
                                    at[:, h, 2 * q:2 * q + 2, :].rearrange("p c w -> p (c w)"), ident[:, :])
                            m.then_inc(s["at_turned"], 1)
                            since(pe, s["hT"], i, h, 1)
                            pe.wait_ge(s["aT"], k0 + 1)
                            for r in range(2):
                                m = nc.tensor.matmul(psH[:, r * 512:(r + 1) * 512], fw1[r * PW:(r + 1) * PW, :],
                                                     aT[r * PW:(r + 1) * PW, :], start=True, stop=True)
                            m.then_inc(s["hidden"], 1)
                            since(pe, s["done"], i, h, 2)
                            pe.wait_ge(s["hT"], k0 + 1)
                            for j in range(CH):
                                at_ = (j % 2) * 512 + (j // 2) * P
                                nc.tensor.matmul(psW[h % 2][:, j, :], hT[:, at_:at_ + P], fw2[:, :],
                                                 start=True, stop=False)
                                m = nc.tensor.matmul(psW[h % 2][:, j, :], ones[0:1, :], fb2[:, :],
                                                     start=False, stop=True)
                            m.then_inc(s["filters"], 1)

                        each(pe, CHUNKS, SLOTS, step)

        def carry_pass(layer, tag, states):
            k = 1 if layer == 2 else 0
            width = {0: W0, 1: D, 2: W2, 3: D}[layer]
            soft = layer in (0, 2)
            heads = NH if layer == 2 else 1
            hw = {0: D + 1, 1: D, 2: HD + 1, 3: D}[layer]
            mcol = {0: D + 2, 2: NH * (HD + 1)}.get(layer)
            used = heads * hw
            with semaphores(nc) as sem, ExitStack() as ctx:
                def sb(n, shape):
                    return ctx.enter_context(nc.sbuf_tensor(f"{tag}_{n}", shape, F32))

                L = sb("L", [P, width])
                val, valT = sb("val", [P, heads, P]), sb("valT", [P, heads, P])
                best, both, ex = sb("best", [P, heads]), sb("both", [P, heads]), sb("ex", [P, 2, heads])
                C = sb("C", [P, used])
                psM = ctx.enter_context(nc.psum_tensor(f"{tag}_psM", [P, heads, P], F32))
                psV = ctx.enter_context(nc.psum_tensor(f"{tag}_psV", [P, heads, P], F32))
                psC = ctx.enter_context(nc.psum_tensor(f"{tag}_psC", [P, 512], F32))
                s = {n: sem(f"{tag}_{n}") for n in (
                    "maxima", "exponents", "exps", "weights", "turned", "valT", "summed", "ready", "none",
                    "got", "scales", "scaled", "stored")}
                block = ctx.enter_context(nc.Block())

                @block.sync
                def _(sp):
                    sp.dma_start(states[EP:EP + P, :], zeros[:, 0:width]).then_inc(s["none"], 16)
                    sp.wait_ge(s["none"], 16)

                @block.gpsimd
                def _(pool):
                    pool.wait_ge(s["none"], 16)
                    nc.gpsimd.indirect_dma_start(
                        out=L[:, :], out_offset=None, in_=states[:, :],
                        in_offset=bass.IndirectOffsetOnAxis(ap=carryi[k][:, 0:1], axis=0)).then_inc(s["got"], 16)
                    pool.wait_ge(s["ready"], 1)
                    nc.gpsimd.indirect_dma_start(
                        out=states[:, :], out_offset=bass.IndirectOffsetOnAxis(ap=carryi[k][:, 0:1], axis=0),
                        in_=L[:, :], in_offset=None).then_inc(s["stored"], 16)
                    pool.wait_ge(s["stored"], 16)

                @block.vector
                def _(dve):
                    v = nc.vector
                    if not soft:
                        dve.wait_ge(s["got"], 16)
                        dve.wait_ge(s["summed"], 1)
                        v.tensor_tensor(L[:, :], L[:, :], psC[:, 0:used], ALU.add).then_inc(s["ready"], 1)
                        return
                    dve.wait_ge(s["maxima"], 1)
                    v.tensor_tensor(val[:, :, :], psM[:, :, :], over(shut[k][:, :], heads), ALU.add)
                    v.drain()
                    v.tensor_reduce(best[:, :], val[:, :, :], AX.X, ALU.max)
                    v.drain()
                    v.tensor_tensor(val[:, :, :], val[:, :, :], along(best[:, :], P),
                                    ALU.subtract).then_inc(s["exponents"], 1)
                    dve.wait_ge(s["exps"], 1)
                    v.tensor_tensor(val[:, :, :], val[:, :, :], over(goesT[k][:, :], heads),
                                    ALU.mult).then_inc(s["weights"], 1)
                    dve.wait_ge(s["turned"], 1)
                    v.tensor_copy(valT[:, :, :], psV[:, :, :]).then_inc(s["valT"], 1)
                    dve.wait_ge(s["got"], 16)
                    v.tensor_tensor(both[:, :], L[:, mcol:mcol + heads], best[:, :], ALU.max)
                    v.drain()
                    v.tensor_tensor(ex[:, 0, :], L[:, mcol:mcol + heads], both[:, :], ALU.subtract)
                    v.tensor_tensor(ex[:, 1, :], best[:, :], both[:, :], ALU.subtract).then_inc(s["scales"], 1)
                    dve.wait_ge(s["scaled"], 1)
                    dve.wait_ge(s["summed"], 1)
                    Lh = L[:, 0:used].rearrange("p (h d) -> p h d", h=heads)
                    Ch = C[:, :].rearrange("p (h d) -> p h d", h=heads)
                    v.tensor_tensor(Lh, Lh, along(ex[:, 0, :], hw), ALU.mult)
                    v.tensor_tensor(Ch, psC[:, 0:used].rearrange("p (h d) -> p h d", h=heads),
                                    along(ex[:, 1, :], hw), ALU.mult)
                    v.drain()
                    v.tensor_tensor(L[:, 0:used], L[:, 0:used], C[:, :], ALU.add).then_inc(s["ready"], 1)

                @block.scalar
                def _(act):
                    if soft:
                        act.wait_ge(s["exponents"], 1)
                        nc.scalar.activation(val[:, :, :], val[:, :, :], ACT.Exp).then_inc(s["exps"], 1)
                        act.wait_ge(s["scales"], 1)
                        nc.scalar.activation(ex[:, :, :], ex[:, :, :], ACT.Exp).then_inc(s["scaled"], 1)

                @block.tensor
                def _(pe):
                    if not soft:
                        nc.tensor.matmul(psC[:, 0:hw], goes[k][:, :], ends[:, 0:hw], start=True,
                                         stop=True).then_inc(s["summed"], 1)
                        return
                    for h in range(heads):
                        m = nc.tensor.matmul(psM[:, h, :], ends[:, mcol + h:mcol + h + 1].to_broadcast([P, P]),
                                             ident[:, :], start=True, stop=True)
                    m.then_inc(s["maxima"], 1)
                    pe.wait_ge(s["weights"], 1)
                    for h in range(heads):
                        m = nc.tensor.transpose(psV[:, h, :], val[:, h, :], ident[:, :])
                    m.then_inc(s["turned"], 1)
                    pe.wait_ge(s["valT"], 1)
                    for h in range(heads):
                        m = nc.tensor.matmul(psC[:, h * hw:(h + 1) * hw], valT[:, h, :], ends[:, h * hw:(h + 1) * hw],
                                             start=True, stop=True)
                    m.then_inc(s["summed"], 1)

        def node_pass(tag, layer=None, states=None, hidden=None, dense=None, width=D,
                      norm=None, table=None, relu=False):
            k = 1 if layer == 2 else 0
            sw = {0: W0, 1: D, 2: W2, 3: D, None: 1}[layer]
            soft = layer in (0, 2)
            heads = NH if layer == 2 else 1
            hw = {0: D + 1, 2: HD + 1}.get(layer)
            per = 512 // width
            tw = table.shape[1] if table is not None else 1
            with semaphores(nc) as sem, ExitStack() as ctx:
                def sb(n, shape, dt=F32):
                    return ctx.enter_context(nc.sbuf_tensor(f"{tag}_{n}", shape, dt))

                S = sb("S", [P, 2, GB, sw])
                ix = sb("ix", [P, 2, GB], I32)
                A = sb("A", [P, 2, GB, D])
                AT = sb("AT", [P, GB * P])
                HT = sb("HT", [P, GB * P])
                OB = sb("OB", [P, 2, GB, tw])
                den = sb("den", [P, GB, heads])
                R = sb("R", [P, 2, GB, D])
                st = sb("st", [P, GB, 6])
                mv = sb("mv", [P, GB, 2])
                sd = sb("sd", [P, GB])
                psT = ctx.enter_context(nc.psum_tensor(f"{tag}_psT", [P, 8 * P], F32))
                psH = ctx.enter_context(nc.psum_tensor(f"{tag}_psH", [P, 8 * P], F32))
                banks = -(-GB // per)
                psO = ctx.enter_context(nc.psum_tensor(f"{tag}_psO", [P, banks, 512], F32))
                s = {n: sem(f"{tag}_{n}") for n in (
                    "ix", "go", "A", "flipped", "AT", "hid", "HT", "out", "sunk",
                    "var", "std", "OB", "x")}
                got = [sem(f"{tag}_got{h}") for h in range(2)]
                stored = [sem(f"{tag}_stored{h}") for h in range(2)]
                block = ctx.enter_context(nc.Block())

                def since(eng, sem, i, h, back):
                    if not (isinstance(i, int) and i * 2 + h < back):
                        eng.wait_ge(sem, i * 2 + h + 1 - back)

                def pieces():
                    for b in range(banks):
                        n = min(per, GB - b * per)
                        yield b * per, n, psO[:, b, 0:n * width].rearrange("p (j w) -> p j w", j=n)

                if layer is not None:
                    @block.gpsimd
                    def _(pool):
                        def step(i, h):
                            since(pool, s["A"], i, h, 2)
                            pool.wait_ge(s["ix"], i * 2 + h + 1)
                            pool.sem_inc(s["go"], 1)
                            for j in range(GB):
                                nc.gpsimd.indirect_dma_start(
                                    out=S[:, h, j, :], out_offset=None, in_=states[:, :],
                                    in_offset=bass.IndirectOffsetOnAxis(ap=ix[:, h, j:j + 1], axis=0)
                                ).then_inc(got[h], 16)

                        each(pool, GROUPS, 2, step)

                @block.scalar
                def _(act):
                    def step(i, h):
                        k0 = i * 2 + h
                        if layer is None:
                            since(act, s["flipped"], i, h, 2)
                            nc.scalar.copy(A[:, h], X[:, bass.ds(k0 * GB, GB), :]).then_inc(s["A"], 1)
                        if dense is not None:
                            act.wait_ge(s["flipped"], k0 + 1)
                            nc.scalar.copy(AT[:, :], psT[:, 0:GB * P]).then_inc(s["AT"], 1)
                        if hidden is not None:
                            act.wait_ge(s["hid"], k0 + 1)
                            nc.scalar.activation(HT[:, :], psH[:, 0:GB * P], ACT.Silu,
                                                 bias=hidden[1][:, 0:1]).then_inc(s["HT"], 1)
                        if norm is not None:
                            act.wait_ge(s["var"], k0 + 1)
                            nc.scalar.activation(sd[:, :], sd[:, :], ACT.Sqrt).then_inc(s["std"], 1)

                    each(act, GROUPS, 2, step)

                if dense is not None:
                    @block.tensor
                    def _(pe):
                        def step(i, h):
                            k0 = i * 2 + h
                            since(pe, s["AT"], i, h, 1)
                            pe.wait_ge(s["A"], k0 + 1)
                            for j in range(GB):
                                m = nc.tensor.transpose(psT[:, j * P:(j + 1) * P], A[:, h, j, :], ident[:, :])
                            m.then_inc(s["flipped"], 1)
                            cols = AT
                            if hidden is not None:
                                since(pe, s["HT"], i, h, 1)
                                pe.wait_ge(s["AT"], k0 + 1)
                                for c0, c1 in ((0, 512), (512, GB * P)):
                                    m = nc.tensor.matmul(psH[:, c0:c1], hidden[0][:, :], AT[:, c0:c1],
                                                         start=True, stop=True)
                                m.then_inc(s["hid"], 1)
                                cols = HT
                            since(pe, s["sunk"], i, h, 1)
                            pe.wait_ge(s["HT" if hidden is not None else "AT"], k0 + 1)
                            for b0, n, ps in pieces():
                                for j in range(n):
                                    at_ = (b0 + j) * P
                                    m = nc.tensor.matmul(ps[:, j, :], cols[:, at_:at_ + P], dense[0][:, :],
                                                         start=True, stop=dense[1] is None)
                                    if dense[1] is not None:
                                        m = nc.tensor.matmul(ps[:, j, :], ones[0:1, :], dense[1][:, :],
                                                             start=False, stop=True)
                            m.then_inc(s["out"], 1)

                        each(pe, GROUPS, 2, step)

                @block.vector
                def _(dve):
                    v = nc.vector
                    if table is not None:
                        v.memset(OB[:, :, :, :], 0.0)
                        v.drain()
                        if table is T0:
                            v.memset(OB[:, :, :, D:D + 1], 1.0)
                        if table is TKV:
                            for h in range(2):
                                v.memset(OB[:, h, :, D:].rearrange("p j (h d) -> p j h d", h=NH)[:, :, :, HD], 1.0)
                        v.drain()

                    def indices(i, h):
                        k0 = i * 2 + h
                        again(dve, got[h], i, 16 * GB)
                        v.tensor_copy(ix[:, h, :], endi[k][:, bass.ds(k0 * GB, GB)]).then_inc(s["ix"], 1)

                    def combine(i, h):
                        k0 = i * 2 + h
                        dve.wait_ge(got[h], 16 * GB * (i + 1))
                        if not (isinstance(i, int) and i * 2 + h + 2 >= GROUPS):
                            indices(i + 1, h)
                        if dense is not None:
                            since(dve, s["flipped"], i, h, 2)
                        hs = has[k][:, bass.ds(k0 * GB, GB)]
                        if not soft:
                            v.tensor_tensor(A[:, h], S[:, h], along(hs, D), ALU.mult).then_inc(s["A"], 1)
                            return
                        used = heads * hw
                        v.tensor_tensor(S[:, h, :, 0:used], S[:, h, :, 0:used], along(hs, used), ALU.mult)
                        v.drain()
                        w = S[:, h, :, 0:heads * hw].rearrange("p j (h d) -> p j h d", h=heads)
                        if layer == 0:
                            v.tensor_scalar(den[:, :, :], w[:, :, :, hw - 1], 1e-8, None, ALU.add)
                        else:
                            v.tensor_tensor(den[:, :, :], w[:, :, :, hw - 1], along(hs, heads), ALU.subtract)
                            v.drain()
                            v.tensor_scalar(den[:, :, :], den[:, :, :], 1.0, None, ALU.add)
                        v.drain()
                        v.reciprocal(den[:, :, :], den[:, :, :])
                        v.drain()
                        v.tensor_tensor(A[:, h].rearrange("p j (h d) -> p j h d", h=heads), w[:, :, :, 0:hw - 1],
                                        den[:, :, :].unsqueeze(3).to_broadcast([P, GB, heads, hw - 1]),
                                        ALU.mult).then_inc(s["A"], 1)
                        v.drain()

                    def sink(i, h):
                        k0 = i * 2 + h
                        xs = X[:, bass.ds(k0 * GB, GB), :]
                        if dense is not None:
                            dve.wait_ge(s["out"], k0 + 1)
                        if table is not None and norm is None:
                            again(dve, stored[h], i, 16)
                            for b0, n, ps in pieces():
                                js = slice(b0, b0 + n)
                                if table is T0:
                                    v.tensor_copy(OB[:, h, js, 0:D], ps[:, :, 0:D])
                                    v.tensor_copy(OB[:, h, js, D + 1:D + 2], ps[:, :, D:D + 1])
                                    m = v.tensor_copy(AD[:, bass.ds(k0 * GB + b0, n)], ps[:, :, D + 1])
                                elif table is TKV:
                                    v.tensor_copy(OB[:, h, js, 0:D], ps[:, :, 0:D])
                                    for j in range(n):
                                        m = v.tensor_copy(
                                            OB[:, h, b0 + j, D:].rearrange("p (h d) -> p h d", h=NH)[:, :, 0:HD],
                                            ps[:, j, D:2 * D].rearrange("p (h d) -> p h d", h=NH))
                                elif relu:
                                    m = v.tensor_scalar(OB[:, h, js, :], ps, 0.0, None, ALU.max)
                                else:
                                    m = v.tensor_copy(OB[:, h, js, :], ps)
                            m.then_inc(s["sunk"], 1)
                            return
                        if norm == "out" or table is not None:
                            again(dve, stored[h], i, 16)
                        if dense is not None:
                            for b0, n, ps in pieces():
                                js = slice(b0, b0 + n)
                                m = v.tensor_tensor(R[:, h, js, :], ps, X[:, bass.ds(k0 * GB + b0, n), :], ALU.add)
                            m.then_inc(s["sunk"], 1)
                            if norm == "out":
                                v.drain()
                                v.tensor_tensor(R[:, h], R[:, h], xs, ALU.add)
                        else:
                            v.tensor_tensor(R[:, h], A[:, h], xs, ALU.add)
                        v.drain()
                        for j in range(GB):
                            v.bn_stats(st[:, j, :], R[:, h, j, :])
                        v.drain()
                        for j in range(GB):
                            v.bn_aggr(mv[:, j, :], st[:, j, :])
                        v.drain()
                        v.tensor_scalar(sd[:, :], mv[:, :, 1], 1e-5, None, ALU.add).then_inc(s["var"], 1)
                        dve.wait_ge(s["std"], k0 + 1)
                        v.reciprocal(sd[:, :], sd[:, :])
                        v.drain()
                        for j in range(GB):
                            m = v.tensor_scalar(R[:, h, j, :], R[:, h, j, :], mv[:, j, 0:1], sd[:, j:j + 1],
                                                ALU.subtract, ALU.mult)
                        if norm != "out":
                            v.drain()
                            m = v.tensor_copy(xs, R[:, h])
                        m.then_inc(s["x"], 1)
                        v.drain()

                    def step(i, h, last=False):
                        if layer is not None and not last:
                            i1, h1 = i + (h + 1) // 2, (h + 1) % 2
                            combine(i1, h1)
                        sink(i, h)

                    if layer is not None:
                        indices(0, 0)
                        indices(0, 1)
                        combine(0, 0)
                    each(dve, GROUPS - 1, 2, step)
                    step((GROUPS - 1) // 2, (GROUPS - 1) % 2, last=True)

                @block.sync
                def _(sp):
                    done = s["sunk"] if norm is None else s["x"]

                    def step(i, h, last=False):
                        k0 = i * 2 + h
                        sp.wait_ge(done, k0 + 1)
                        of = R[:, h] if norm is not None else OB[:, h]
                        if norm == "out" and last:
                            b0 = (GROUPS - 1) * GB
                            sp.dma_start(out[b0 * P:(NB - 1) * P].rearrange("(b p) f -> p b f", p=P),
                                         of[:, 0:GB - 1, :]).then_inc(stored[h], 16)
                            sp.dma_start(out[(NB - 1) * P:N], of[0:N - (NB - 1) * P, GB - 1, :]).then_inc(stored[h], 16)
                        else:
                            to = out[0:(NB - 1) * P] if norm == "out" else table
                            sp.dma_start(to.rearrange("(b p) f -> p b f", p=P)[:, bass.ds(k0 * GB, GB), :],
                                         of).then_inc(stored[h], 16)

                    if table is not None or norm == "out":
                        each(sp, GROUPS - 1, 2, step)
                        step((GROUPS - 1) // 2, (GROUPS - 1) % 2, last=True)
                        sp.wait_ge(stored[0], 16 * (GROUPS // 2 + 1) + (16 if norm == "out" else 0))
                        sp.wait_ge(stored[1], 16 * (GROUPS // 2))

        with ExitStack() as early:
            inkeys = (early.enter_context(nc.sbuf_tensor("inputs", [P, NC, 4], F32)),
                      [early.enter_context(nc.sbuf_tensor(f"hi{k}", [P, NC], BF16)) for k in range(2)],
                      [early.enter_context(nc.sbuf_tensor(f"lo{k}", [P, NC], BF16)) for k in range(2)],
                      early.enter_context(nc.sbuf_tensor("scores", [P, NC, 2 + NH], F32)))
            setup(inkeys)
            count_edges(inkeys)
            sort_edges(inkeys)
        node_pass("n0", dense=(w0, None), width=D + 2, table=T0)
        order_edges()
        spread_ad()
        edge_pass(0, "e0", T0, S0)
        carry_pass(0, "c0", S0)
        node_pass("f0", layer=0, states=S0, norm=True, table=T1)
        edge_pass(1, "e1", T1, S1)
        carry_pass(1, "c1", S1)
        node_pass("f1", layer=1, states=S1, dense=(w1[0], None), relu=True, table=TH)
        edge_pass(1, "e2", TH, S1)
        carry_pass(1, "c2", S1)
        node_pass("f2", layer=1, states=S1, dense=(w1[1], None), norm=True)
        node_pass("nq", dense=(wq, bq), table=TQ)
        node_pass("nk", dense=(wkv, bkv), width=2 * D, table=TKV)
        edge_pass(2, "e3", TKV, S2)
        carry_pass(2, "c3", S2)
        node_pass("f3", layer=2, states=S2, dense=(wo, bo), norm=True)
        node_pass("n3", hidden=(aw1, ab1), dense=(aw2, ab2), table=T3)
        edge_pass(3, "e4", T3, S1)
        carry_pass(3, "c4", S1)
        node_pass("f4", layer=3, states=S1, hidden=(ow1, ob1), dense=(ow2, ob2), norm="out")


_IN = ["x", "src", "dst", "edge_attr_128", "edge_attr_50", "edge_weight", "edge_weight_n2", "L0_gnn_W", "L0_gnn_a",
       "L1_gnn_W0", "L1_gnn_W1", "L2_gnn_Wq", "L2_gnn_bq", "L2_gnn_Wk", "L2_gnn_bk", "L2_gnn_Wv", "L2_gnn_bv",
       "L2_gnn_We", "L2_gnn_be", "L2_gnn_Wo", "L2_gnn_bo", "L3_gnn_fw1", "L3_gnn_fb1", "L3_gnn_fw2", "L3_gnn_fb2",
       "L3_gnn_aw1", "L3_gnn_ab1", "L3_gnn_aw2", "L3_gnn_ab2", "L3_gnn_ow1", "L3_gnn_ob1", "L3_gnn_ow2",
       "L3_gnn_ob2"]


def kernel(**inputs):
    import numpy as np
    import concourse.bacc as bacc
    from concourse.bass_utils import run_bass_kernel_spmd

    nc = bacc.Bacc("TRN2", target_bir_lowering=False, num_devices=1)
    arrays = {f"in_{n}": np.ascontiguousarray(inputs[n]) for n in _IN}
    t = {n: nc.dram_tensor(f"in_{n}", arrays[f"in_{n}"].shape, mybir.dt.from_np(arrays[f"in_{n}"].dtype),
                           kind="ExternalInput").ap() for n in _IN}
    out = nc.dram_tensor("out", (N, D), F32, kind="ExternalOutput").ap()
    gnn(nc, t, out)
    return run_bass_kernel_spmd(nc, [arrays], core_ids=[0]).results[0]["out"]
```

```python
import concourse.bass as bass
from concourse import mybir
from contextlib import ExitStack, contextmanager

P = 128
D = 128
N = 6250
E = 106250
NG = 50
NH, HD = 8, 16
NB = -(-N // P)
NN = NB * P
CH = 8
NC = 832
EP = P * NC
CHUNKS = NC // CH
FULLC = E // P
REST = E - P * FULLC
SLOTS = 4
PW = 64
SW = 16
W0 = 132
W2 = 144
KVW = D + NH * (HD + 1)
BIG = 1e30
GB = 7
GROUPS = NB // GB

F32, BF16, I32 = mybir.dt.float32, mybir.dt.bfloat16, mybir.dt.int32
ALU = mybir.AluOpType
ACT = mybir.ActivationFunctionType
AX = mybir.AxisListType


@contextmanager
def semaphores(nc):
    held = []

    def sem(name):
        held.append(nc.alloc_semaphore(name=name))
        return held[-1]

    yield sem
    nc.all_engine_barrier()
    nc.clear_and_free_semaphores(held)
    nc.all_engine_barrier()


def each(eng, total, slots, body, tail=0, head=True):
    rounds = (total - tail) // slots
    if head:
        for h in range(slots):
            body(0, h)
    with eng.Fori(1 if head else 0, rounds) as i:
        for h in range(slots):
            body(i, h)
    for k in range(rounds * slots, total):
        body(k // slots, k % slots)


def again(eng, sem, i, unit):
    if not (isinstance(i, int) and i == 0):
        eng.wait_ge(sem, i * unit)


def over(a, n):
    return a.unsqueeze(1).to_broadcast([a.shape[0], n, a.shape[1]])


def along(a, n):
    return a.unsqueeze(2).to_broadcast([a.shape[0], a.shape[1], n])


def gnn(nc, t, out):
    top = ExitStack()
    with top:
        def keep(name, shape, dt=F32):
            return top.enter_context(nc.sbuf_tensor(name, shape, dt))

        def dram(name, shape):
            return nc.dram_tensor(name, shape, F32, kind="Internal").ap()

        X = keep("X", [P, NB, D])
        ident = keep("ident", [P, P])
        identb = keep("identb", [P, P], BF16)
        later = keep("later", [P, P])
        iota = keep("iota", [P, P], BF16)
        part = keep("part", [P, 1])
        ones = keep("ones", [P, P])
        zeros = keep("zeros", [P, 256])
        base = [keep(f"base{k}", [P, NB]) for k in range(2)]
        count = [keep(f"count{k}", [P, NB]) for k in range(2)]
        has = [keep(f"has{k}", [P, NB]) for k in range(2)]
        endi = [keep(f"endi{k}", [P, NB + 2 * GB], I32) for k in range(2)]
        carryi = [keep(f"carryi{k}", [P, 1], I32) for k in range(2)]
        goes = [keep(f"goes{k}", [P, P]) for k in range(2)]
        goesT = [keep(f"goesT{k}", [P, P]) for k in range(2)]
        shut = [keep(f"shut{k}", [P, P]) for k in range(2)]
        ends = keep("ends", [P, W2])
        firsti = keep("firsti", [P, 1], I32)
        firstq = keep("firstq", [P, 1], I32)
        starti = keep("starti", [P, NB], I32)
        startq = keep("startq", [P, NB], I32)
        Qfirst = keep("Qfirst", [P, D])
        key = [keep(f"key{k}", [P, NC]) for k in range(2)]
        mixed = keep("mixed", [1, 1], I32)
        AD = keep("AD", [P, NB])

        NS = NC + 2 * CH
        src_d = keep("src_d", [P, NS], I32)
        meta_d = keep("meta_d", [P, NS, 5])
        dst_s = keep("dst_s", [P, NS], I32)
        src_s = keep("src_s", [P, NS], I32)
        meta_s = keep("meta_s", [P, NS, 2 + NH])

        w0 = keep("w0", [P, D + 2])
        w1 = [keep(f"w1_{k}", [P, D]) for k in range(2)]
        wq, wkv, we, wo = keep("wq", [P, D]), keep("wkv", [P, 2 * D]), keep("we", [P, NH]), keep("wo", [P, D])
        bq, bkv, bo = keep("bq", [P, D]), keep("bkv", [P, 2 * D]), keep("bo", [P, D])
        be = keep("be", [P, NH])
        fw1 = keep("fw1", [P, D])
        fw2, aw1, aw2, ow1, ow2 = (keep(n, [P, D]) for n in ("fw2", "aw1", "aw2", "ow1", "ow2"))
        fb1, ab1, ob1 = (keep(n, [P, 1]) for n in ("fb1", "ab1", "ob1"))
        fb2, ab2, ob2 = (keep(n, [P, D]) for n in ("fb2", "ab2", "ob2"))

        T0, T1, TQ = dram("T0", (NN, W0)), dram("T1", (NN, D)), dram("TQ", (NN, D))
        TH, T3, TKV = dram("TH", (NN, D)), dram("T3", (NN, D)), dram("TKV", (NN, KVW))
        ADT = dram("ADT", (NN, 1))
        sorted_d, sorted_s = dram("sorted_d", (EP, PW)), dram("sorted_s", (EP, SW))
        ADE = dram("ADE", (EP + P, 1))
        QE = dram("QE", (EP + P, D))
        S0, S1, S2 = (dram(f"S{k}", (EP + P, w)) for k, w in enumerate((W0, D, W2)))

        def setup(inkeys):
            with semaphores(nc) as sem, ExitStack() as ctx:
                col_i = ctx.enter_context(nc.sbuf_tensor("col_i", [P, P], I32))
                part_i = ctx.enter_context(nc.sbuf_tensor("part_i", [P, 1], I32))
                colf = ctx.enter_context(nc.sbuf_tensor("colf", [P, P], F32))
                raw = ctx.enter_context(nc.sbuf_tensor("raw", [P, 3, D], F32))
                acol = ctx.enter_context(nc.sbuf_tensor("acol", [P, 2], F32))
                keys = [ctx.enter_context(nc.sbuf_tensor(f"keys{k}", [P, NC], I32)) for k in range(2)]
                cut = ctx.enter_context(nc.sbuf_tensor("cut", [P, NC], I32))
                ew2 = ctx.enter_context(nc.sbuf_tensor("ew2", [P, NC], F32))
                ew1 = ctx.enter_context(nc.sbuf_tensor("ew1", [P, NC], F32))
                psT = ctx.enter_context(nc.psum_tensor("psT", [P, 3, D], F32))
                psA = ctx.enter_context(nc.psum_tensor("psA", [P, 2], F32))
                psF = ctx.enter_context(nc.psum_tensor("psF", [1, 1], F32))
                given = [ctx.enter_context(nc.sbuf_tensor(f"given{m}", [P, NC], I32)) for m in range(3)]
                wgt = [ctx.enter_context(nc.sbuf_tensor(f"wgt{m}", [P, NC], F32)) for m in range(2)]
                rising = ctx.enter_context(nc.sbuf_tensor("rising", [P, NC], F32))
                risen = ctx.enter_context(nc.sbuf_tensor("risen", [P, 1], F32))
                iotas, cleared, loaded, consts, wT, risen_all, a01 = (
                    sem(n)
                    for n in ("iotas", "cleared", "loaded", "consts", "wT", "risen", "a01"))
                block = ctx.enter_context(nc.Block())
                loads = [
                    (X[:, 0:NB - 1, :], t["x"][0:(NB - 1) * P].rearrange("(b p) f -> p b f", p=P)),
                    (X[0:N - (NB - 1) * P, NB - 1, :], t["x"][(NB - 1) * P:N]),
                    (raw[:, 0, :], t["L0_gnn_W"]), (raw[:, 1, :], t["L1_gnn_W0"]), (raw[:, 2, :], t["L1_gnn_W1"]),
                    (acol[:, 0:1], t["L0_gnn_a"][0, 0:D].unsqueeze(1)),
                    (acol[:, 1:2], t["L0_gnn_a"][0, D:2 * D].unsqueeze(1)),
                    (wq[:, :], t["L2_gnn_Wq"]), (wkv[:, 0:D], t["L2_gnn_Wk"]), (wkv[:, D:2 * D], t["L2_gnn_Wv"]),
                    (we[:, :], t["L2_gnn_We"]), (wo[:, :], t["L2_gnn_Wo"]),
                    (bq[:, :], t["L2_gnn_bq"].unsqueeze(0).to_broadcast([P, D])), (bkv[:, 0:D], t["L2_gnn_bk"].unsqueeze(0).to_broadcast([P, D])),
                    (bkv[:, D:2 * D], t["L2_gnn_bv"].unsqueeze(0).to_broadcast([P, D])), (bo[:, :], t["L2_gnn_bo"].unsqueeze(0).to_broadcast([P, D])),
                    (be[:, :], t["L2_gnn_be"].unsqueeze(0).to_broadcast([P, NH])),
                    (fw1[4:4 + NG, :], t["L3_gnn_fw1"]), (fw1[PW + 4:PW + 4 + NG, :], t["L3_gnn_fw1"]),
                    (fw2[:, :], t["L3_gnn_fw2"]), (aw1[:, :], t["L3_gnn_aw1"]), (aw2[:, :], t["L3_gnn_aw2"]),
                    (ow1[:, :], t["L3_gnn_ow1"]), (ow2[:, :], t["L3_gnn_ow2"]),
                    (fb1[:, :], t["L3_gnn_fb1"].unsqueeze(1)), (ab1[:, :], t["L3_gnn_ab1"].unsqueeze(1)),
                    (ob1[:, :], t["L3_gnn_ob1"].unsqueeze(1)), (fb2[:, :], t["L3_gnn_fb2"].unsqueeze(0).to_broadcast([P, D])),
                    (ab2[:, :], t["L3_gnn_ab2"].unsqueeze(0).to_broadcast([P, D])), (ob2[:, :], t["L3_gnn_ob2"].unsqueeze(0).to_broadcast([P, D])),
                ]
                for tile, name in ((keys[0], "dst"), (keys[1], "src"), (ew1, "edge_weight"), (ew2, "edge_weight_n2")):
                    loads.append((tile[:, 0:FULLC], t[name][0:P * FULLC].rearrange("(p c) -> p c", p=P)))
                    loads.append((tile[0:REST, FULLC:FULLC + 1], t[name][P * FULLC:E].unsqueeze(1)))

                tail = E - (P - 1) * NC
                for tile, name, at_ in ((given[0], "dst", 0), (given[1], "src", 0), (given[2], "dst", 1),
                                        (wgt[0], "edge_weight", 0), (wgt[1], "edge_weight_n2", 0)):
                    loads.append((tile[0:P - 1, :], t[name][at_:at_ + (P - 1) * NC].rearrange("(p c) -> p c", c=NC)))
                    loads.append((tile[P - 1:P, 0:tail - at_], t[name][at_ + (P - 1) * NC:E].unsqueeze(0)))

                @block.sync
                def _(sp):
                    sp.wait_ge(cleared, 13)
                    for to, of in loads:
                        sp.dma_start(to, of).then_inc(loaded, 16)

                @block.gpsimd
                def _(pool):
                    nc.gpsimd.iota(col_i[:, :], pattern=[[1, P]], base=0, channel_multiplier=0).then_inc(iotas, 1)
                    nc.gpsimd.iota(part_i[:, :], pattern=[[0, 1]], base=0, channel_multiplier=1).then_inc(iotas, 1)

                @block.vector
                def _(dve):
                    v = nc.vector
                    v.memset(X[:, NB - 1, :], 0.0).then_inc(cleared, 1)
                    v.memset(fw1[:, :], 0.0).then_inc(cleared, 1)
                    v.memset(keys[0][:, FULLC:NC], N).then_inc(cleared, 1)
                    v.memset(keys[1][:, FULLC:NC], N).then_inc(cleared, 1)
                    v.memset(ew1[:, FULLC:NC], 0.0).then_inc(cleared, 1)
                    v.memset(ew2[:, FULLC:NC], 0.0).then_inc(cleared, 1)
                    for m in range(3):
                        v.memset(given[m][:, tail - 1:NC], N).then_inc(cleared, 1)
                    for m in range(2):
                        v.memset(wgt[m][:, tail:NC], 0.0).then_inc(cleared, 1)
                    v.memset(zeros[:, :], 0.0).then_inc(cleared, 1)
                    v.memset(ones[:, :], 1.0).then_inc(cleared, 1)
                    for k in range(2):
                        v.memset(endi[k][:, NB:], 0)
                    for m in (src_d, dst_s, src_s):
                        v.memset(m[:, NC:NS], 0)
                    v.memset(meta_d[:, NC:NS, :], 0.0)
                    v.memset(meta_s[:, NC:NS, :], 0.0)
                    dve.wait_ge(iotas, 2)
                    v.tensor_copy(colf[:, :], col_i[:, :])
                    v.tensor_copy(iota[:, :], col_i[:, :])
                    v.tensor_copy(part[:, :], part_i[:, :])
                    v.drain()
                    v.tensor_scalar(ident[:, :], colf[:, :], part[:, 0:1], None, ALU.is_equal)
                    v.tensor_scalar(later[:, :], colf[:, :], part[:, 0:1], None, ALU.is_gt)
                    v.drain()
                    v.tensor_copy(identb[:, :], ident[:, :]).then_inc(consts, 1)
                    dve.wait_ge(loaded, 16 * len(loads))
                    v.tensor_scalar(wq[:, :], wq[:, :], HD ** -0.5, None, ALU.mult)
                    v.tensor_scalar(bq[:, :], bq[:, :], HD ** -0.5, None, ALU.mult)
                    v.tensor_copy(src_d[:, 0:NC], given[1][:, :])
                    v.tensor_copy(key[0][:, :], given[0][:, :])
                    v.tensor_copy(meta_d[:, 0:NC, 2], wgt[0][:, :])
                    v.tensor_tensor(meta_d[:, 0:NC, 4], wgt[0][:, :], wgt[1][:, :], ALU.mult)
                    v.tensor_tensor(rising[:, :], given[2][:, :], given[0][:, :], ALU.is_ge)
                    v.drain()
                    v.tensor_reduce(risen[:, :], rising[:, :], AX.X, ALU.min)
                    v.drain().then_inc(risen_all, 1)
                    inputs, hi, lo, scores = inkeys
                    v.tensor_copy(inputs[:, :, 0], keys[1][:, :])
                    v.tensor_copy(inputs[:, :, 1], ew1[:, :])
                    v.tensor_tensor(inputs[:, :, 2], ew1[:, :], ew2[:, :], ALU.mult)
                    v.tensor_copy(inputs[:, :, 3], keys[0][:, :])
                    v.tensor_copy(scores[:, :, 0], keys[0][:, :])
                    v.tensor_copy(scores[:, :, 1], keys[1][:, :])
                    for k in range(2):
                        v.drain()
                        v.tensor_scalar(cut[:, :], keys[k][:, :], 7, None, ALU.logical_shift_right)
                        v.drain()
                        v.tensor_copy(hi[k][:, :], cut[:, :])
                        v.drain()
                        v.tensor_scalar(cut[:, :], keys[k][:, :], P - 1, None, ALU.bitwise_and)
                        v.drain()
                        v.tensor_copy(lo[k][:, :], cut[:, :])
                    dve.wait_ge(wT, 1)
                    v.tensor_copy(w0[:, 0:D], psT[:, 0, :])
                    v.tensor_copy(w1[0][:, :], psT[:, 1, :])
                    v.tensor_copy(w1[1][:, :], psT[:, 2, :])
                    dve.wait_ge(a01, 1)
                    v.tensor_copy(w0[:, D:D + 2], psA[:, :])
                    v.tensor_scalar(mixed[:, :], psF[:, :], float(P), None, ALU.is_lt)

                @block.tensor
                def _(pe):
                    pe.wait_ge(consts, 1)
                    pe.wait_ge(loaded, 16 * len(loads))
                    for k in range(3):
                        m = nc.tensor.transpose(psT[:, k, :], raw[:, k, :], ident[:, :])
                    m.then_inc(wT, 1)
                    pe.wait_ge(risen_all, 1)
                    nc.tensor.matmul(psF[:, :], risen[:, :], ones[:, 0:1], start=True, stop=True)
                    nc.tensor.matmul(psA[:, :], raw[:, 0, :], acol[:, :], start=True, stop=True).then_inc(a01, 1)

        def attr_loads(sp, source, width, dst, slots, free, unit, ready, rest):
            view = source[0:P * FULLC].rearrange("(p c) f -> p c f", p=P)

            def step(i, h):
                again(sp, free[h], i, unit)
                sp.dma_start(dst(h), view[:, bass.ds((i * slots + h) * CH, CH), :]).then_inc(ready[h], 16)

            each(sp, CHUNKS - 1, slots, step)
            c0, h = NC - CH, (CHUNKS - 1) % slots
            again(sp, free[h], (CHUNKS - 1) // slots, unit)
            whole = FULLC - c0
            d = dst(h)
            sp.dma_start(d[0:REST, whole, :], source[P * FULLC:E]).then_inc(rest, 16)
            sp.dma_start(d[REST:P, whole, :], zeros[REST:P, 0:width]).then_inc(rest, 16)
            sp.dma_start(d[:, whole + 1, :], zeros[:, 0:width]).then_inc(rest, 16)
            sp.wait_ge(rest, 48)
            sp.dma_start(d[:, 0:whole, :], view[:, c0:FULLC, :]).then_inc(ready[h], 16)

        def count_edges(inkeys):
            inputs, hi, lo, scores = inkeys
            with semaphores(nc) as sem, ExitStack() as ctx:
                ea = ctx.enter_context(nc.sbuf_tensor("ea", [P, 4, CH, D], F32))
                eaT = ctx.enter_context(nc.sbuf_tensor("eaT", [P, 2, CH * P], F32))
                B = ctx.enter_context(nc.sbuf_tensor("Bc", [P, 2, 2, CH, P], BF16))
                A = ctx.enter_context(nc.sbuf_tensor("Ac", [P, 2, 2, CH, NB], BF16))
                zb = ctx.enter_context(nc.sbuf_tensor("zb", [P, P], BF16))
                sums = ctx.enter_context(nc.sbuf_tensor("sums", [P, 2, NB], F32))
                psE = [ctx.enter_context(nc.psum_tensor(f"psE{h}", [P, CH * P], F32)) for h in range(2)]
                psS = [ctx.enter_context(nc.psum_tensor(f"psS{h}", [P, CH, NH], F32)) for h in range(2)]
                psC = [ctx.enter_context(nc.psum_tensor(f"psC{k}", [P, 512], F32)) for k in range(2)]
                s = {n: sem(n) for n in (
                    "ea_rest", "hot", "counted", "flipped",
                    "eaT_ready", "scored", "score_kept", "zb_ready", "all_counted", "between", "total")}
                ea_ready = [sem(f"ea_ready{h}") for h in range(4)]
                ea_free = [sem(f"ea_free{h}") for h in range(4)]
                block = ctx.enter_context(nc.Block())

                @block.sync
                def _(sp):
                    attr_loads(sp, t["edge_attr_128"], D, lambda h: ea[:, h], 4, ea_free, 1, ea_ready, s["ea_rest"])

                @block.vector
                def _(dve):
                    v = nc.vector
                    v.memset(zb[:, :], 0.0).then_inc(s["zb_ready"], 1)

                    def hot(i, h):
                        k0 = i * 2 + h
                        if not (isinstance(k0, int) and k0 < 2):
                            dve.wait_ge(s["counted"], k0 - 1)
                        for k in range(2):
                            v.tensor_tensor(A[:, h, k], over(iota[:, 0:NB], CH),
                                            along(hi[k][:, bass.ds(k0 * CH, CH)], NB), ALU.is_equal)
                            m = v.tensor_tensor(B[:, h, k], over(iota[:, :], CH),
                                                along(lo[k][:, bass.ds(k0 * CH, CH)], P), ALU.is_equal)
                        m.then_inc(s["hot"], 1)

                    def score(i, h):
                        k0 = i * 2 + h
                        dve.wait_ge(s["scored"], k0 + 1)
                        v.tensor_tensor(scores[:, bass.ds(k0 * CH, CH), 2:2 + NH], psS[h][:, :, :],
                                        over(be[:, :], CH), ALU.add).then_inc(s["score_kept"], 1)

                    def step(i, h):
                        hot(i + (h + 1) // 2, (h + 1) % 2)
                        score(i, h)

                    hot(0, 0)
                    each(dve, CHUNKS - 1, 2, step)
                    score((CHUNKS - 1) // 2, (CHUNKS - 1) % 2)
                    dve.wait_ge(s["all_counted"], 1)
                    for k in range(2):
                        v.tensor_copy(count[k][:, :], psC[k][:, 0:NB])
                    v.drain()
                    for k in range(2):
                        v.tensor_scalar(has[k][:, :], count[k][:, :], 1.0, None, ALU.min)
                    v.memset(sums[:, :, :], 0.0).then_inc(s["total"], 1)
                    dve.wait_ge(s["between"], 1)
                    for k in range(2):
                        v.tensor_tensor_scan(sums[:, k, 1:NB], ones[:, 0:NB - 1], psE[0][:, k * P:k * P + NB - 1],
                                             0.0, ALU.mult, ALU.add)
                    v.drain()
                    for k in range(2):
                        v.tensor_tensor(base[k][:, :], sums[:, k, :], psE[1][:, k * P:k * P + NB], ALU.add)

                @block.scalar
                def _(act):
                    def step(i, h):
                        k0 = i * 4 + h
                        if not (isinstance(k0, int) and k0 < 2):
                            act.wait_ge(s["scored"], k0 - 1)
                        act.wait_ge(s["flipped"], k0 + 1)
                        nc.scalar.copy(eaT[:, h % 2, :], psE[h % 2][:, :]).then_inc(s["eaT_ready"], 1)
                        act.sem_inc(ea_free[h], 1)

                    each(act, CHUNKS, 4, step)

                @block.tensor
                def _(pe):
                    pe.wait_ge(s["zb_ready"], 1)
                    for k in range(2):
                        nc.tensor.matmul(psC[k][:, 0:NB], zb[:, :], zb[:, 0:NB], start=True, stop=False)

                    def flip(i, h):
                        k0 = i * 4 + h
                        if not (isinstance(k0, int) and k0 < 2):
                            pe.wait_ge(s["eaT_ready"], k0 - 1)
                        pe.wait_ge(ea_ready[h], 16 * (i + 1))
                        for j in range(CH):
                            m = nc.tensor.transpose(psE[h % 2][:, j * P:(j + 1) * P], ea[:, h, j, :], ident[:, :])
                        m.then_inc(s["flipped"], 1)

                    def step(i, h, last=False):
                        k0, h2 = i * 4 + h, h % 2
                        if not last:
                            flip(i + (h + 1) // 4, (h + 1) % 4)
                        pe.wait_ge(s["hot"], k0 + 1)
                        for j in range(CH):
                            for k in range(2):
                                m = nc.tensor.matmul(psC[k][:, 0:NB], B[:, h2, k, j, :], A[:, h2, k, j, :],
                                                     start=False, stop=False)
                        m.then_inc(s["counted"], 1)
                        if not (isinstance(k0, int) and k0 < 2):
                            pe.wait_ge(s["score_kept"], k0 - 1)
                        pe.wait_ge(s["eaT_ready"], k0 + 1)
                        for j in range(CH):
                            m = nc.tensor.matmul(psS[h2][:, j, :], eaT[:, h2, j * P:(j + 1) * P], we[:, :],
                                                 start=True, stop=True)
                        m.then_inc(s["scored"], 1)

                    flip(0, 0)
                    each(pe, CHUNKS - 1, 4, step)
                    step((CHUNKS - 1) // 4, (CHUNKS - 1) % 4, last=True)
                    for k in range(2):
                        m = nc.tensor.matmul(psC[k][:, 0:NB], zb[:, :], zb[:, 0:NB], start=False, stop=True)
                    m.then_inc(s["all_counted"], 1)
                    pe.wait_ge(s["total"], 1)
                    for k in range(2):
                        nc.tensor.matmul(psE[0][:, k * P:k * P + NB], ones[:, :], count[k][:, :], start=True, stop=True)
                        m = nc.tensor.matmul(psE[1][:, k * P:k * P + NB], later[:, :], count[k][:, :],
                                             start=True, stop=True)
                    m.then_inc(s["between"], 1)

        def sort_edges(inkeys, order):
            inputs, hi, lo, scores = inkeys
            k, tag = order, "ds"[order]
            rw, table = ((PW, sorted_d), (SW, sorted_s))[k]
            fields, nfield = ((inputs, 4), (scores, 2 + NH))[k]
            SL = 4
            with semaphores(nc) as sem, ExitStack() as ctx:
                def sb(n, shape, dt=F32):
                    return ctx.enter_context(nc.sbuf_tensor(f"so{tag}_{n}", shape, dt))

                B = sb("B", [P, SL, CH, P], BF16)
                A = sb("A", [P, SL, CH, NB], BF16)
                BT = sb("BT", [P, 2, CH * P])
                M = sb("M", [P, 2, CH, P], BF16)
                run = sb("run", [P, CH, NB])
                hit = sb("hit", [P, CH, NB])
                posf = sb("posf", [P, CH])
                pos = sb("pos", [P, SL, CH], I32)
                rec = sb("rec", [P, SL, CH, rw])
                psB = ctx.enter_context(nc.psum_tensor(f"so{tag}_psB", [P, CH * P], BF16))
                psG = ctx.enter_context(nc.psum_tensor(f"so{tag}_psG", [P, 512], F32))
                psR = [ctx.enter_context(nc.psum_tensor(f"so{tag}_psR{a}", [P, 512], F32)) for a in range(2)]
                psQ = [ctx.enter_context(nc.psum_tensor(f"so{tag}_psQ{h}", [P, CH, P], F32)) for h in range(2)]
                ranks = psG[:, 0:CH * NB].rearrange("p (j b) -> p j b", j=CH)
                s = {n: sem(f"so{tag}_{n}") for n in (
                    "cleared", "rest", "hot", "flipped", "BT", "alike", "masked", "added", "run", "ranked",
                    "placed", "fields", "go")}
                sent = [sem(f"so{tag}_sent{h}") for h in range(SL)]
                attrs = [sem(f"so{tag}_attrs{h}") for h in range(SL)] if k == 0 else None
                block = ctx.enter_context(nc.Block())

                def since(eng, sem_, i, h, back):
                    if not (isinstance(i, int) and i * SL + h < back):
                        eng.wait_ge(sem_, i * SL + h + 1 - back)

                def ahead(i, h, n):
                    return i + (h + n) // SL, (h + n) % SL

                if k == 0:
                    @block.sync
                    def _(sp):
                        sp.wait_ge(s["cleared"], 1)
                        attr_loads(sp, t["edge_attr_50"], NG, lambda h: rec[:, h, :, 4:4 + NG], SL,
                                   sent, 16 * CH, attrs, s["rest"])

                @block.gpsimd
                def _(pool):
                    def step(i, h):
                        pool.wait_ge(s["placed"], i * SL + h + 1)
                        if k == 0:
                            pool.wait_ge(attrs[h], 16 * (i + 1))
                        pool.wait_ge(s["fields"], i * SL + h + 1)
                        pool.sem_inc(s["go"], 1)
                        for j in range(CH):
                            nc.gpsimd.indirect_dma_start(
                                out=table[:, :], out_offset=bass.IndirectOffsetOnAxis(ap=pos[:, h, j:j + 1], axis=0),
                                in_=rec[:, h, j, :], in_offset=None).then_inc(sent[h], 16)

                    each(pool, CHUNKS, SL, step)
                    for h in range(SL):
                        pool.wait_ge(sent[h], 16 * CH * (CHUNKS // SL))

                @block.vector
                def _(dve):
                    v = nc.vector
                    v.memset(rec[:, :, :, :], 0.0).then_inc(s["cleared"], 1)

                    def hot(i, h):
                        k0 = i * SL + h
                        since(dve, s["ranked"], i, h, SL)
                        v.tensor_tensor(A[:, h], over(iota[:, 0:NB], CH),
                                        along(hi[k][:, bass.ds(k0 * CH, CH)], NB), ALU.is_equal)
                        v.tensor_tensor(B[:, h], over(iota[:, :], CH),
                                        along(lo[k][:, bass.ds(k0 * CH, CH)], P), ALU.is_equal).then_inc(s["hot"], 1)

                    def mask(i, h):
                        since(dve, s["ranked"], i, h, 2)
                        dve.wait_ge(s["alike"], i * SL + h + 1)
                        v.tensor_tensor(M[:, h % 2], psQ[h % 2][:, :, :], over(later[:, :], CH),
                                        ALU.mult).then_inc(s["masked"], 1)

                    def place(i, h):
                        dve.wait_ge(s["ranked"], i * SL + h + 1)
                        v.tensor_tensor(hit[:, :, :], ranks, A[:, h], ALU.mult)
                        v.drain()
                        v.tensor_reduce(posf[:, :], hit[:, :, :], AX.X, ALU.add)
                        v.drain()
                        again(dve, sent[h], i, 16 * CH)
                        v.tensor_copy(pos[:, h, :], posf[:, :]).then_inc(s["placed"], 1)

                    hot(0, 0)
                    mask(0, 0)
                    hot(0, 1)

                    def step(i, h):
                        mask(*ahead(i, h, 1))
                        hot(*ahead(i, h, 2))
                        place(i, h)

                    each(dve, CHUNKS - 2, SL, step)
                    mask((CHUNKS - 1) // SL, (CHUNKS - 1) % SL)
                    for c in (CHUNKS - 2, CHUNKS - 1):
                        place(c // SL, c % SL)

                @block.scalar
                def _(act):
                    act.wait_ge(s["added"], 1)
                    nc.scalar.copy(run[:, 0, :], psR[0][:, 0:NB]).then_inc(s["run"], 1)
                    act.wait_ge(s["cleared"], 1)

                    def turned(i, h):
                        since(act, s["ranked"], i, h, 2)
                        act.wait_ge(s["flipped"], i * SL + h + 1)
                        nc.scalar.copy(BT[:, h % 2, :], psB[:, :]).then_inc(s["BT"], 1)

                    def count_(i, h):
                        k0 = i * SL + h
                        again(act, sent[h], i, 16 * CH)
                        nc.scalar.copy(rec[:, h, :, 0:nfield], fields[:, bass.ds(k0 * CH, CH), :]).then_inc(
                            s["fields"], 1)
                        for j in range(CH):
                            act.wait_ge(s["added"], k0 * CH + j + 2)
                            nc.scalar.copy(run[:, (j + 1) % CH, :], psR[(j + 1) % 2][:, 0:NB]).then_inc(s["run"], 1)

                    turned(0, 0)

                    def step(i, h):
                        turned(*ahead(i, h, 1))
                        count_(i, h)

                    each(act, CHUNKS - 1, SL, step)
                    count_((CHUNKS - 1) // SL, (CHUNKS - 1) % SL)

                @block.tensor
                def _(pe):
                    for a in range(2):
                        m = nc.tensor.matmul(psR[a][:, 0:NB], ident[:, :], base[k][:, :], start=True, stop=True)
                    m.then_inc(s["added"], 1)

                    def compare(i, h):
                        k0 = i * SL + h
                        since(pe, s["BT"], i, h, 1)
                        pe.wait_ge(s["hot"], k0 + 1)
                        for j in range(CH):
                            m = nc.tensor.transpose(psB[:, j * P:(j + 1) * P], B[:, h, j, :], identb[:, :])
                        m.then_inc(s["flipped"], 1)
                        since(pe, s["masked"], i, h, 2)
                        pe.wait_ge(s["BT"], k0 + 1)
                        for j in range(CH):
                            b = BT[:, h % 2, j * P:(j + 1) * P]
                            m = nc.tensor.matmul(psQ[h % 2][:, j, :], b, b, start=True, stop=True)
                        m.then_inc(s["alike"], 1)

                    def rank(i, h):
                        k0 = i * SL + h
                        since(pe, s["placed"], i, h, 1)
                        pe.wait_ge(s["masked"], k0 + 1)
                        for j in range(CH):
                            other = psR[(j + 1) % 2][:, 0:NB]
                            if not (isinstance(k0, int) and k0 + j == 0):
                                pe.wait_ge(s["run"], k0 * CH + j)
                                hl, jl = (h, j - 1) if j else ((h - 1) % SL, CH - 1)
                                nc.tensor.matmul(other, B[:, hl, jl, :], A[:, hl, jl, :], start=False,
                                                 stop=True, skip_group_check=True)
                            nc.tensor.matmul(other, B[:, h, j, :], A[:, h, j, :], start=False,
                                             stop=True, skip_group_check=True).then_inc(s["added"], 1)
                            pe.wait_ge(s["run"], k0 * CH + j + 1)
                            nc.tensor.matmul(ranks[:, j, :], BT[:, h % 2, j * P:(j + 1) * P], run[:, j, :],
                                             start=True, stop=False)
                            m = nc.tensor.matmul(ranks[:, j, :], M[:, h % 2, j, :], A[:, h, j, :],
                                                 start=False, stop=True)
                        m.then_inc(s["ranked"], 1)

                    compare(0, 0)

                    def step(i, h):
                        compare(*ahead(i, h, 1))
                        rank(i, h)

                    each(pe, CHUNKS - 1, SL, step)
                    rank((CHUNKS - 1) // SL, (CHUNKS - 1) % SL)

        def take(order):
            tag = "ds"[order]
            GC, rw, table = NC // 16, (PW, SW)[order], (sorted_d, sorted_s)[order]
            with semaphores(nc) as sem, ExitStack() as ctx:
                r = ctx.enter_context(nc.sbuf_tensor(f"rec{tag}", [P, 2, GC, rw], F32))
                landed = [sem(f"landed{tag}{h}") for h in range(2)]
                taken = sem(f"taken{tag}")
                block = ctx.enter_context(nc.Block())

                @block.sync
                def _(sp):
                    for g in range(16):
                        if g > 1:
                            sp.wait_ge(taken, g - 1)
                        sp.dma_start(r[:, g % 2], table.rearrange("(p c) w -> p c w", p=P)[
                            :, g * GC:(g + 1) * GC, :]).then_inc(landed[g % 2], 16)

                @block.vector
                def _(dve):
                    v = nc.vector
                    for g in range(16):
                        dve.wait_ge(landed[g % 2], 16 * (g // 2 + 1))
                        cs, f = slice(g * GC, (g + 1) * GC), r[:, g % 2]
                        if order == 0:
                            v.tensor_copy(src_d[:, cs], f[:, :, 0])
                            v.tensor_copy(meta_d[:, cs, 2], f[:, :, 1])
                            v.tensor_copy(meta_d[:, cs, 4], f[:, :, 2])
                            v.tensor_copy(key[0][:, cs], f[:, :, 3]).then_inc(taken, 1)
                        else:
                            v.tensor_copy(dst_s[:, cs], f[:, :, 0])
                            v.tensor_copy(src_s[:, cs], f[:, :, 1])
                            v.tensor_copy(key[1][:, cs], f[:, :, 1])
                            v.tensor_copy(meta_s[:, cs, 2:2 + NH], f[:, :, 2:2 + NH]).then_inc(taken, 1)

        def order_edges():
            with semaphores(nc) as sem, ExitStack() as ctx:
                alike = ctx.enter_context(nc.sbuf_tensor("alike", [P, NC], F32))
                run = ctx.enter_context(nc.sbuf_tensor("run", [P, 1], F32))
                flag = ctx.enter_context(nc.sbuf_tensor("flag", [P, 4], F32))
                last = ctx.enter_context(nc.sbuf_tensor("last", [P, NB], F32))
                past = ctx.enter_context(nc.sbuf_tensor("past", [P, 1], F32))
                psK = [ctx.enter_context(nc.psum_tensor(f"psK{k}", [P, P], F32)) for k in range(4)]
                s = {n: sem("or_" + n) for n in (
                    "keys", "firsts", "goes", "turned")}
                block = ctx.enter_context(nc.Block())

                @block.vector
                def _(dve):
                    v = nc.vector
                    v.drain().then_inc(s["keys"], 1)
                    for k, meta in ((0, meta_d), (1, meta_s)):
                        v.memset(meta[:, 0:1, 0], 0.0)
                        v.tensor_tensor(meta[:, 1:NC, 0], key[k][:, 1:NC], key[k][:, 0:NC - 1], ALU.is_equal)
                        v.drain()
                        v.tensor_scalar(meta[:, 0:NC, 1], meta[:, 0:NC, 0], 1.0, BIG, ALU.subtract, ALU.mult)
                        v.tensor_tensor(last[:, :], base[k][:, :], count[k][:, :], ALU.add)
                        v.drain()
                        v.tensor_scalar(last[:, :], last[:, :], -1.0, None, ALU.add)
                        v.drain()
                        v.tensor_scalar(endi[k][:, 0:NB], last[:, :], 0.0, None, ALU.max)
                    dve.wait_ge(s["firsts"], 1)
                    for k in range(2):
                        v.scalar_tensor_tensor(out=goes[k][:, :], in0=psK[k][:, :], scalar=key[k][:, NC - 1:NC],
                                               in1=later[:, :], op0=ALU.is_equal, op1=ALU.mult)
                    v.drain().then_inc(s["goes"], 1)
                    dve.wait_ge(s["turned"], 1)
                    for k in range(2):
                        v.tensor_copy(goesT[k][:, :], psK[2 + k][:, :])
                        v.tensor_scalar(shut[k][:, :], psK[2 + k][:, :], 1.0, BIG, ALU.subtract, ALU.mult)
                    v.tensor_copy(firsti[:, :], key[0][:, 0:1])
                    v.tensor_copy(firstq[:, :], key[1][:, 0:1])
                    v.tensor_scalar(past[:, :], part[:, :], float(EP), None, ALU.add)
                    v.drain()
                    for k in range(2):
                        v.tensor_scalar(alike[:, :], key[k][:, :], key[k][:, 0:1], None, ALU.is_equal)
                        v.tensor_reduce(flag[:, 0:1], goesT[k][:, :], AX.X, ALU.max)
                        v.tensor_reduce(flag[:, 1:2], goes[k][:, :], AX.X, ALU.max)
                        v.drain()
                        v.tensor_reduce(run[:, :], alike[:, :], AX.X, ALU.add)
                        v.drain()
                        v.tensor_scalar(flag[:, 2:3], run[:, :], float(NC), None, ALU.is_ge)
                        v.drain()
                        v.tensor_tensor(flag[:, 2:3], flag[:, 2:3], flag[:, 1:2], ALU.mult)
                        v.drain()
                        v.tensor_tensor(flag[:, 0:1], flag[:, 0:1], flag[:, 2:3], ALU.is_gt)
                        v.scalar_tensor_tensor(out=flag[:, 3:4], in0=part[:, :], scalar=float(NC - 1), in1=run[:, :],
                                               op0=ALU.mult, op1=ALU.add)
                        v.drain()
                        v.tensor_scalar(flag[:, 3:4], flag[:, 3:4], float(-1 - EP), None, ALU.add)
                        v.drain()
                        v.tensor_tensor(flag[:, 3:4], flag[:, 3:4], flag[:, 0:1], ALU.mult)
                        v.drain()
                        v.tensor_tensor(carryi[k][:, :], flag[:, 3:4], past[:, :], ALU.add)
                    for k, start in ((0, starti), (1, startq)):
                        v.tensor_scalar(last[:, :], base[k][:, :], past[:, :], None, ALU.subtract)
                        v.drain()
                        v.tensor_tensor(last[:, :], last[:, :], has[k][:, :], ALU.mult)
                        v.drain()
                        v.tensor_scalar(start[:, :], last[:, :], past[:, :], None, ALU.add)
                        v.drain()

                @block.tensor
                def _(pe):
                    pe.wait_ge(s["keys"], 1)
                    for k in range(2):
                        m = nc.tensor.matmul(psK[k][:, :], key[k][:, 0:1].to_broadcast([P, P]), ident[:, :],
                                             start=True, stop=True)
                    m.then_inc(s["firsts"], 1)
                    pe.wait_ge(s["goes"], 1)
                    for k in range(2):
                        m = nc.tensor.transpose(psK[2 + k][:, :], goes[k][:, :], ident[:, :])
                    m.then_inc(s["turned"], 1)

        def spread_ad():
            with semaphores(nc) as sem, ExitStack() as ctx:
                sown = ctx.enter_context(nc.sbuf_tensor("sown", [P, NC], F32))
                filled = ctx.enter_context(nc.sbuf_tensor("filled", [P, NC], F32))
                same = ctx.enter_context(nc.sbuf_tensor("same", [P, NC], F32))
                first = ctx.enter_context(nc.sbuf_tensor("first", [P, 1], F32))
                s = {n: sem("ad_" + n) for n in ("zeroed", "written", "sown", "first",
                                                                            "back", "clear")}
                block = ctx.enter_context(nc.Block())

                @block.vector
                def _(dve):
                    v = nc.vector
                    v.memset(filled[:, :], 0.0).then_inc(s["clear"], 1)
                    v.tensor_copy(same[:, :], meta_d[:, 0:NC, 0])
                    dve.wait_ge(s["back"], 16)
                    dve.wait_ge(s["first"], 16)
                    dve.wait_ge(s["zeroed"], 16)
                    v.tensor_copy(sown[:, 0:1], first[:, :])
                    v.drain()
                    v.tensor_tensor_scan(filled[:, :], same[:, :], sown[:, :], 0.0, ALU.mult, ALU.add)
                    v.drain()
                    v.tensor_copy(meta_d[:, 0:NC, 3], filled[:, :])

                @block.sync
                def _(sp):
                    sp.wait_ge(s["clear"], 1)
                    sp.dma_start(ADE[0:EP].rearrange("(p c) w -> p (c w)", p=P), filled[:, :]).then_inc(s["zeroed"], 16)
                    with nc.allow_non_contiguous_dma(reason="a column of a node table"):
                        sp.dma_start(ADT.rearrange("(b p) w -> p (b w)", p=P), AD[:, :]).then_inc(s["written"], 16)
                    sp.wait_ge(s["sown"], 16 * NB)
                    sp.dma_start(sown[:, :], ADE[0:EP].rearrange("(p c) w -> p (c w)", p=P)).then_inc(s["back"], 16)

                @block.gpsimd
                def _(pool):
                    pool.wait_ge(s["zeroed"], 16)
                    for b in range(NB):
                        nc.gpsimd.indirect_dma_start(
                            out=ADE[:, :], out_offset=bass.IndirectOffsetOnAxis(ap=starti[:, b:b + 1], axis=0),
                            in_=AD[:, b:b + 1], in_offset=None).then_inc(s["sown"], 16)
                    pool.wait_ge(s["written"], 16)
                    nc.gpsimd.indirect_dma_start(
                        out=first[:, :], out_offset=None, in_=ADT[:, :],
                        in_offset=bass.IndirectOffsetOnAxis(ap=firsti[:, 0:1], axis=0)).then_inc(s["first"], 16)

        EARLY = 2
        ZEROING = "e1"

        def edge_pass(layer, tag, table, states):
            soft = layer in (0, 2)
            k = 1 if layer == 2 else 0
            meta = (meta_d, meta_s)[k]
            nf = meta[:, 0:1, :].shape[2]
            width = {0: W0, 1: D, 2: W2, 3: D}[layer]
            used = {0: D + 1, 1: D, 2: NH * (HD + 1), 3: D}[layer]
            heads = NH if layer == 2 else 1
            gathers = [(table, KVW if layer == 2 else table.shape[1], dst_s if layer == 2 else src_d)]
            with semaphores(nc) as sem, ExitStack() as ctx:
                def sb(n, shape, dt=F32):
                    return ctx.enter_context(nc.sbuf_tensor(f"{tag}_{n}", shape, dt))

                got_rows = [sb(f"rows{m}", [P, SLOTS, CH, w]) for m, (_, w, _) in enumerate(gathers)]
                G = got_rows[0]
                ix = sb("ix", [P, len(gathers), SLOTS, CH], I32)
                mb = sb("mb", [P, SLOTS, CH, nf])
                O = sb("O", [P, SLOTS, CH, width])
                top_ = sb("top", [P, SLOTS, CH + 1, heads])
                sc = sb("sc", [P, SLOTS, 3, CH, heads])
                coef = sb("coef", [P, SLOTS, 2, CH, heads])
                if layer == 2:
                    prod = sb("prod", [P, CH, D])
                    Q = sb("Q", [P, SLOTS, CH, D])
                    q_here = [sem(f"{tag}_q{h}") for h in range(SLOTS)]
                if tag == ZEROING:
                    blank = sb("blank", [P, CH, D])
                if layer == 3:
                    at = sb("at", [P, SLOTS, CH, PW])
                    aT = sb("aT", [P, CH // 2 * P])
                    filt = sb("filt", [P, CH, D])
                    hT = sb("hT", [P, 2, CH * P])
                    psT = ctx.enter_context(nc.psum_tensor(f"{tag}_psT", [P, CH // 2 * P], F32))
                    psH = ctx.enter_context(nc.psum_tensor(f"{tag}_psH", [P, CH * P], F32))
                    psW = [ctx.enter_context(nc.psum_tensor(f"{tag}_psW{h}", [P, CH, P], F32)) for h in range(2)]
                s = {n: sem(f"{tag}_{n}") for n in (
                    "fields", "go", "done", "clear", "blank", "blanked", "diffs", "coefs", "messages", "at_turned", "aT", "hidden",
                    "hT", "filters")}
                got = [sem(f"{tag}_got{h}") for h in range(SLOTS)]
                stored = [sem(f"{tag}_stored{h}") for h in range(SLOTS)]
                at_here = [sem(f"{tag}_at{h}") for h in range(SLOTS)]
                at_last = [sem(f"{tag}_al{h}") for h in range(SLOTS)]
                unit = 16 * CH * len(gathers)
                block = ctx.enter_context(nc.Block())

                def since(eng, sem, i, h, back):
                    if not (isinstance(i, int) and i * SLOTS + h < back):
                        eng.wait_ge(sem, i * SLOTS + h + 1 - back)

                def after(i, h, n):
                    return i + (h + n) // SLOTS, (h + n) % SLOTS

                @block.gpsimd
                def _(pool):
                    def step(i, h):
                        since(pool, s["done"], i, h, SLOTS)
                        pool.wait_ge(s["fields"], i * SLOTS + h + 1)
                        pool.sem_inc(s["go"], 1)
                        for j in range(CH):
                            for m, (tab, w, _) in enumerate(gathers):
                                nc.gpsimd.indirect_dma_start(
                                    out=got_rows[m][:, h, j, :], out_offset=None, in_=tab[:, :],
                                    in_offset=bass.IndirectOffsetOnAxis(ap=ix[:, m, h, j:j + 1], axis=0)
                                ).then_inc(got[h], 16)

                    each(pool, CHUNKS, SLOTS, step)

                @block.sync
                def _(sp):
                    sview = states[0:EP].rearrange("(p c) w -> p c w", p=P)
                    cut, whole = divmod(E - (P - 1) * NC, CH)

                    def sorted_load(c, k0, h):
                        sp.dma_start(at[:, h, :, 4:4 + NG], sorted_d.rearrange("(p c) w -> p c w", p=P)[
                            :, bass.ds(k0 * CH, CH), 4:4 + NG]).then_inc(at_here[h], 16)

                    def given_load(c, k0, h):
                        src_ = t["edge_attr_50"]
                        rows = src_[0:(P - 1) * NC].rearrange("(p c) w -> p c w", c=NC)
                        if c is None or c < cut:
                            last = src_[(P - 1) * NC:(P - 1) * NC + cut * CH].unsqueeze(0)
                            sp.dma_start(at[P - 1:P, h, :, 4:4 + NG], last[:, bass.ds(k0 * CH, CH), :]).then_inc(
                                at_last[h], 16)
                        else:
                            n = whole if c == cut else 1
                            last = src_[(P - 1) * NC + cut * CH:(P - 1) * NC + cut * CH + n].unsqueeze(0)
                            sp.dma_start(at[P - 1:P, h, 0:n, 4:4 + NG], last).then_inc(at_last[h], 16)
                        sp.dma_start(at[0:P - 1, h, :, 4:4 + NG], rows[:, bass.ds(k0 * CH, CH), :]).then_inc(
                            at_here[h], 16)

                    qview = QE[0:EP].rearrange("(p c) w -> p c w", p=P)

                    def query_load(c, k0, h):
                        sp.dma_start(Q[:, h, :, :], qview[:, bass.ds(k0 * CH, CH), :]).then_inc(q_here[h], 16)

                    def run(load, lead=2):
                        def fetch(i, h, c=None):
                            since(sp, s["done" if layer == 2 else "at_turned"], i, h, SLOTS)
                            load(c, i * SLOTS + h, h)

                        def step(i, h, c=None):
                            if load is not None and not (c is not None and c + lead >= CHUNKS):
                                fetch(*after(i, h, lead), None if c is None else c + lead)
                            if tag == ZEROING:
                                sp.dma_start(qview[:, bass.ds((i * SLOTS + h) * CH, CH), :],
                                             blank[:, :, :]).then_inc(s["blanked"], 16)
                            sp.wait_ge(s["done"], i * SLOTS + h + 1)
                            sp.dma_start(sview[:, bass.ds((i * SLOTS + h) * CH, CH), :], O[:, h, :, :]).then_inc(
                                stored[h], 16)

                        if load is not None:
                            for h in range(lead):
                                fetch(0, h)
                        first = (cut - 2) // SLOTS * SLOTS if load is given_load else CHUNKS - SLOTS
                        each(sp, first, SLOTS, step)
                        if load is given_load:
                            for c in range(first, first + SLOTS):
                                step(c // SLOTS, c % SLOTS, c)
                            with sp.Fori(first // SLOTS + 1, CHUNKS // SLOTS - 1) as i:
                                for h in range(SLOTS):
                                    step(i, h, cut + 1)
                        for c in range(CHUNKS - SLOTS, CHUNKS):
                            step(c // SLOTS, c % SLOTS, c)

                    if tag == ZEROING:
                        sp.wait_ge(s["blank"], 1)
                    if layer == 2:
                        run(query_load, lead=3)
                    elif layer != 3:
                        run(None)
                    else:
                        sp.wait_ge(s["clear"], 1)
                        with sp.If(sp.value_load(mixed[0:1, 0:1], min_val=0, max_val=1) > 0):
                            for h in range(SLOTS):
                                sp.sem_inc(at_last[h], 16 * (CHUNKS // SLOTS))
                            run(sorted_load)
                        with sp.Else():
                            run(given_load)
                    for h in range(SLOTS):
                        sp.wait_ge(stored[h], 16 * (CHUNKS // SLOTS))
                    if tag == ZEROING:
                        sp.wait_ge(s["blanked"], 16 * CHUNKS)

                @block.scalar
                def _(act):
                    def fetch(i, h, c0):
                        again(act, got[h], i, unit)
                        since(act, s["done"], i, h, SLOTS)
                        for m, (_, _, idx) in enumerate(gathers):
                            nc.scalar.copy(ix[:, m, h, :], idx[:, bass.ds(c0, CH)])
                        nc.scalar.copy(mb[:, h, :, :], meta[:, bass.ds(c0, CH), :]).then_inc(s["fields"], 1)

                    def hidden(i, h):
                        k0 = i * SLOTS + h
                        act.wait_ge(s["at_turned"], k0 + 1)
                        nc.scalar.copy(aT[:, :], psT[:, :]).then_inc(s["aT"], 1)
                        since(act, s["filters"], i, h, 2)
                        act.wait_ge(s["hidden"], k0 + 1)
                        nc.scalar.activation(hT[:, h % 2, :], psH[:, :], ACT.Silu,
                                             bias=fb1[:, 0:1]).then_inc(s["hT"], 1)

                    fetch(0, 0, 0)
                    fetch(0, 1, CH)
                    if layer == 3:
                        hidden(0, 0)

                    def step(i, h):
                        k0 = i * SLOTS + h
                        act.wait_ge(got[h], (i + 1) * unit)
                        fetch(i + (h + 2) // SLOTS, (h + 2) % SLOTS, (k0 + 2) * CH)
                        if layer == 3 and not (isinstance(k0, int) and k0 + 1 >= CHUNKS):
                            hidden(*after(i, h, 1))
                        if layer == 1:
                            act.wait_ge(s["fields"], k0 + 1)
                            for j in range(CH):
                                m = nc.scalar.activation(G[:, h, j, :], G[:, h, j, :], ACT.Copy,
                                                         scale=mb[:, h, j, 4:5])
                            m.then_inc(s["messages"], 1)
                        if soft:
                            act.wait_ge(s["diffs"], k0 + 1)
                            nc.scalar.activation(coef[:, h], sc[:, h, 1:3], ACT.Exp).then_inc(s["coefs"], 1)
                        if layer == 2:
                            act.wait_ge(s["coefs"], k0 + 1)
                            for j in range(EARLY, CH):
                                for n in range(NH):
                                    vs = G[:, h, j, D + n * (HD + 1):D + (n + 1) * (HD + 1)]
                                    m = nc.scalar.activation(vs, vs, ACT.Copy, scale=coef[:, h, 1, j, n:n + 1])
                                m.then_inc(s["messages"], 1)
                        if layer == 0:
                            act.wait_ge(s["coefs"], k0 + 1)
                            for j in range(CH):
                                m = nc.scalar.activation(G[:, h, j, 0:used], G[:, h, j, 0:used], ACT.Copy,
                                                         scale=coef[:, h, 1, j, :])
                            m.then_inc(s["messages"], 1)

                    each(act, CHUNKS, SLOTS, step, tail=1)

                @block.vector
                def _(dve):
                    v = nc.vector
                    if layer == 3:
                        v.memset(at[:, :, :, :], 0.0).then_inc(s["clear"], 1)
                    if tag == ZEROING:
                        v.memset(blank[:, :, :], 0.0).then_inc(s["blank"], 1)
                    v.memset(O[:, :, :, :], 0.0)
                    v.memset(top_[:, :, :, :], 0.0)
                    v.drain()

                    def scores_(i, h):
                        k0, hp = i * SLOTS + h, (h - 1) % SLOTS
                        dve.wait_ge(got[h], (i + 1) * unit)
                        dve.wait_ge(s["fields"], k0 + 1)
                        v.tensor_copy(top_[:, h, 0, :], top_[:, hp, CH, :])
                        a, b = sc[:, h, 0, :, 0], top_[:, h, 1:CH + 1, 0]
                        v.tensor_tensor(a, G[:, h, :, D + 1], mb[:, h, :, 3], ALU.add)
                        v.drain()
                        v.scalar_tensor_tensor(out=a, in0=a, scalar=0.2, in1=a, op0=ALU.mult, op1=ALU.max)
                        v.drain()
                        v.tensor_tensor(a, a, mb[:, h, :, 2], ALU.mult)
                        v.drain()
                        v.tensor_tensor_scan(b, mb[:, h, :, 0], a, top_[:, h, 0, :], ALU.mult, ALU.max)
                        v.drain()
                        exponents(h)

                    def exponents(h):
                        v.tensor_tensor(sc[:, h, 1], top_[:, h, 0:CH, :], along(mb[:, h, :, 1], heads), ALU.add)
                        v.tensor_tensor(sc[:, h, 2], sc[:, h, 0], top_[:, h, 1:CH + 1, :], ALU.subtract)
                        v.drain()
                        v.tensor_tensor(sc[:, h, 1], sc[:, h, 1], top_[:, h, 1:CH + 1, :],
                                        ALU.subtract).then_inc(s["diffs"], 1)

                    def sums(i, h):
                        k0, hp = i * SLOTS + h, (h - 1) % SLOTS
                        if layer in (0, 1):
                            dve.wait_ge(s["messages"], k0 + 1)
                        dve.wait_ge(s["fields"], k0 + 1)
                        if layer == 3:
                            dve.wait_ge(got[h], (i + 1) * unit)
                            dve.wait_ge(s["filters"], k0 + 1)
                            v.tensor_tensor(filt[:, :, :], psW[h % 2][:, :, :], over(fb2[:, :], CH), ALU.add)
                            v.drain()
                            v.tensor_tensor(G[:, h], filt[:, :, :], G[:, h], ALU.mult)
                        if layer == 3:
                            v.drain()
                        again(dve, stored[h], i, 16)
                        if layer == 0:
                            v.tensor_copy(O[:, h, :, D + 2:D + 3], top_[:, h, 1:CH + 1, :])
                        for j in range(CH):
                            before = O[:, hp, CH - 1, 0:used] if j == 0 else O[:, h, j - 1, 0:used]
                            now = O[:, h, j, 0:used]
                            f = coef[:, h, 0, j, :] if layer == 0 else mb[:, h, j, 0:1]
                            m = v.scalar_tensor_tensor(out=now, in0=before, scalar=f, in1=G[:, h, j, 0:used],
                                                       op0=ALU.mult, op1=ALU.add)
                            if j < CH - 1:
                                v.drain()
                        m.then_inc(s["done"], 1)
                        v.drain()

                    def fill(i, h, j):
                        if isinstance(i, int) and i * SLOTS + h + j == 0:
                            v.tensor_copy(Q[:, 0, 0, :], Qfirst[:, :])
                            return
                        before = Q[:, (h - 1) % SLOTS, CH - 1, :] if j == 0 else Q[:, h, j - 1, :]
                        v.scalar_tensor_tensor(out=Q[:, h, j, :], in0=before, scalar=mb[:, h, j, 0:1],
                                               in1=Q[:, h, j, :], op0=ALU.mult, op1=ALU.add)

                    def score(h, part):
                        if part == 0:
                            v.tensor_tensor(prod[:, :, :], G[:, h, :, 0:D], Q[:, h, :, :], ALU.mult)
                        elif part == 1:
                            v.tensor_reduce(sc[:, h, 0, :, :], prod[:, :, :].rearrange("p c (h d) -> p c h d", h=NH),
                                            AX.X, ALU.add)
                        else:
                            v.tensor_tensor(sc[:, h, 0, :, :], sc[:, h, 0, :, :], mb[:, h, :, 2:2 + NH], ALU.add)

                    def rise(h, j):
                        v.scalar_tensor_tensor(out=top_[:, h, j + 1, :], in0=top_[:, h, j, :],
                                               scalar=mb[:, h, j, 1:2], in1=sc[:, h, 0, j, :],
                                               op0=ALU.add, op1=ALU.max)

                    def state(h, half):
                        j, now = half // 2, O[:, h, half // 2, 0:used]
                        if half % 2:
                            return v.tensor_tensor(now, now, G[:, h, j, D:D + used], ALU.add)
                        before = O[:, (h - 1) % SLOTS, CH - 1, 0:used] if j == 0 else O[:, h, j - 1, 0:used]
                        return v.tensor_tensor(now.rearrange("p (h d) -> p h d", h=NH),
                                               before.rearrange("p (h d) -> p h d", h=NH),
                                               along(coef[:, h, 0, j, :], HD + 1), ALU.mult)

                    ALONE = 2

                    def attend(i, h, coming=True, going=True):
                        k0, hs = i * SLOTS + h, (h - 1) % SLOTS
                        if coming:
                            dve.wait_ge(got[h], (i + 1) * unit)
                            dve.wait_ge(s["fields"], k0 + 1)
                            dve.wait_ge(q_here[h], (i + 1) * 16)
                            v.tensor_copy(top_[:, h, 0, :], top_[:, hs, CH, :])
                            for j in range(ALONE):
                                fill(i, h, j)
                                v.drain()
                            fill(i, h, ALONE)
                        if going:
                            dve.wait_ge(s["coefs"], k0)
                            V = G[:, hs, :, D:KVW].rearrange("p c (h d) -> p c h d", h=NH)
                            v.tensor_tensor(V[:, 0:EARLY], V[:, 0:EARLY], coef[:, hs, 1, 0:EARLY].unsqueeze(
                                3).to_broadcast([P, EARLY, NH, HD + 1]), ALU.mult)
                            again(dve, stored[hs], i - 1 if hs == SLOTS - 1 else i, 16)
                            v.tensor_copy(O[:, hs, :, used:used + heads], top_[:, hs, 1:CH + 1, :])
                        v.drain()
                        for n in range(2 * CH):
                            j = n + ALONE + 1
                            if coming and j < CH:
                                fill(i, h, j)
                            elif coming and j < CH + 3:
                                score(h, j - CH)
                            elif coming and j < 2 * CH + 3:
                                rise(h, j - CH - 3)
                            if going:
                                if n % 2 and n // 2 >= EARLY:
                                    dve.wait_ge(s["messages"], (k0 - 1) * (CH - EARLY) + n // 2 - EARLY + 1)
                                m = state(hs, n)
                                if n == 2 * CH - 1:
                                    m.then_inc(s["done"], 1)
                            v.drain()
                        if coming:
                            exponents(h)

                    if layer == 2:
                        attend(0, 0, going=False)
                        each(dve, CHUNKS - 1, SLOTS, lambda i, h: attend(*after(i, h, 1)))
                        attend(CHUNKS // SLOTS, 0, coming=False)
                    elif layer != 0:
                        each(dve, CHUNKS, SLOTS, sums)
                    else:
                        scores_(0, 0)

                        def step(i, h):
                            scores_(i + (h + 1) // SLOTS, (h + 1) % SLOTS)
                            sums(i, h)

                        each(dve, CHUNKS - 1, SLOTS, step)
                        sums((CHUNKS - 1) // SLOTS, (CHUNKS - 1) % SLOTS)
                    v.tensor_copy(ends[:, 0:width], O[:, (CHUNKS - 1) % SLOTS, CH - 1, :])

                if layer == 3:
                    @block.tensor
                    def _(pe):
                        def hidden(i, h):
                            k0 = i * SLOTS + h
                            since(pe, s["aT"], i, h, 1)
                            pe.wait_ge(at_last[h], (i + 1) * 16)
                            pe.wait_ge(at_here[h], (i + 1) * 16)
                            for q in range(CH // 2):
                                m = nc.tensor.transpose(
                                    psT[:, q * P:(q + 1) * P],
                                    at[:, h, 2 * q:2 * q + 2, :].rearrange("p c w -> p (c w)"), ident[:, :])
                            m.then_inc(s["at_turned"], 1)
                            since(pe, s["hT"], i, h, 1)
                            pe.wait_ge(s["aT"], k0 + 1)
                            for r in range(2):
                                m = nc.tensor.matmul(psH[:, r * 512:(r + 1) * 512], fw1[r * PW:(r + 1) * PW, :],
                                                     aT[r * PW:(r + 1) * PW, :], start=True, stop=True)
                            m.then_inc(s["hidden"], 1)

                        def filters(i, h):
                            since(pe, s["done"], i, h, 2)
                            pe.wait_ge(s["hT"], i * SLOTS + h + 1)
                            for j in range(CH):
                                at_ = (j % 2) * 512 + (j // 2) * P
                                m = nc.tensor.matmul(psW[h % 2][:, j, :], hT[:, h % 2, at_:at_ + P], fw2[:, :],
                                                     start=True, stop=True)
                            m.then_inc(s["filters"], 1)

                        def step(i, h):
                            hidden(*after(i, h, 1))
                            filters(i, h)

                        hidden(0, 0)
                        each(pe, CHUNKS - 1, SLOTS, step)
                        filters((CHUNKS - 1) // SLOTS, (CHUNKS - 1) % SLOTS)

        def carry_pass(layer, tag, states):
            k = 1 if layer == 2 else 0
            width = {0: W0, 1: D, 2: W2, 3: D}[layer]
            soft = layer in (0, 2)
            heads = NH if layer == 2 else 1
            hw = {0: D + 1, 1: D, 2: HD + 1, 3: D}[layer]
            mcol = {0: D + 2, 2: NH * (HD + 1)}.get(layer)
            used = heads * hw
            with semaphores(nc) as sem, ExitStack() as ctx:
                def sb(n, shape):
                    return ctx.enter_context(nc.sbuf_tensor(f"{tag}_{n}", shape, F32))

                L = sb("L", [P, width])
                val, valT = sb("val", [P, heads, P]), sb("valT", [P, heads, P])
                best, both, ex = sb("best", [P, heads]), sb("both", [P, heads]), sb("ex", [P, 2, heads])
                C = sb("C", [P, used])
                psM = ctx.enter_context(nc.psum_tensor(f"{tag}_psM", [P, heads, P], F32))
                psV = ctx.enter_context(nc.psum_tensor(f"{tag}_psV", [P, heads, P], F32))
                psC = ctx.enter_context(nc.psum_tensor(f"{tag}_psC", [P, 512], F32))
                s = {n: sem(f"{tag}_{n}") for n in (
                    "maxima", "exponents", "exps", "weights", "turned", "valT", "summed", "ready", "none",
                    "got", "scales", "scaled", "stored")}
                block = ctx.enter_context(nc.Block())

                @block.sync
                def _(sp):
                    sp.dma_start(states[EP:EP + P, :], zeros[:, 0:width]).then_inc(s["none"], 16)
                    sp.wait_ge(s["none"], 16)

                @block.gpsimd
                def _(pool):
                    pool.wait_ge(s["none"], 16)
                    nc.gpsimd.indirect_dma_start(
                        out=L[:, :], out_offset=None, in_=states[:, :],
                        in_offset=bass.IndirectOffsetOnAxis(ap=carryi[k][:, 0:1], axis=0)).then_inc(s["got"], 16)
                    pool.wait_ge(s["ready"], 1)
                    nc.gpsimd.indirect_dma_start(
                        out=states[:, :], out_offset=bass.IndirectOffsetOnAxis(ap=carryi[k][:, 0:1], axis=0),
                        in_=L[:, :], in_offset=None).then_inc(s["stored"], 16)
                    pool.wait_ge(s["stored"], 16)

                @block.vector
                def _(dve):
                    v = nc.vector
                    if not soft:
                        dve.wait_ge(s["got"], 16)
                        dve.wait_ge(s["summed"], 1)
                        v.tensor_tensor(L[:, :], L[:, :], psC[:, 0:used], ALU.add).then_inc(s["ready"], 1)
                        return
                    dve.wait_ge(s["maxima"], 1)
                    v.tensor_tensor(val[:, :, :], psM[:, :, :], over(shut[k][:, :], heads), ALU.add)
                    v.drain()
                    v.tensor_reduce(best[:, :], val[:, :, :], AX.X, ALU.max)
                    v.drain()
                    v.tensor_tensor(val[:, :, :], val[:, :, :], along(best[:, :], P),
                                    ALU.subtract).then_inc(s["exponents"], 1)
                    dve.wait_ge(s["exps"], 1)
                    v.tensor_tensor(val[:, :, :], val[:, :, :], over(goesT[k][:, :], heads),
                                    ALU.mult).then_inc(s["weights"], 1)
                    dve.wait_ge(s["turned"], 1)
                    v.tensor_copy(valT[:, :, :], psV[:, :, :]).then_inc(s["valT"], 1)
                    dve.wait_ge(s["got"], 16)
                    v.tensor_tensor(both[:, :], L[:, mcol:mcol + heads], best[:, :], ALU.max)
                    v.drain()
                    v.tensor_tensor(ex[:, 0, :], L[:, mcol:mcol + heads], both[:, :], ALU.subtract)
                    v.tensor_tensor(ex[:, 1, :], best[:, :], both[:, :], ALU.subtract).then_inc(s["scales"], 1)
                    dve.wait_ge(s["scaled"], 1)
                    dve.wait_ge(s["summed"], 1)
                    Lh = L[:, 0:used].rearrange("p (h d) -> p h d", h=heads)
                    Ch = C[:, :].rearrange("p (h d) -> p h d", h=heads)
                    v.tensor_tensor(Lh, Lh, along(ex[:, 0, :], hw), ALU.mult)
                    v.tensor_tensor(Ch, psC[:, 0:used].rearrange("p (h d) -> p h d", h=heads),
                                    along(ex[:, 1, :], hw), ALU.mult)
                    v.drain()
                    v.tensor_tensor(L[:, 0:used], L[:, 0:used], C[:, :], ALU.add).then_inc(s["ready"], 1)

                @block.scalar
                def _(act):
                    if soft:
                        act.wait_ge(s["exponents"], 1)
                        nc.scalar.activation(val[:, :, :], val[:, :, :], ACT.Exp).then_inc(s["exps"], 1)
                        act.wait_ge(s["scales"], 1)
                        nc.scalar.activation(ex[:, :, :], ex[:, :, :], ACT.Exp).then_inc(s["scaled"], 1)

                @block.tensor
                def _(pe):
                    if not soft:
                        nc.tensor.matmul(psC[:, 0:hw], goes[k][:, :], ends[:, 0:hw], start=True,
                                         stop=True).then_inc(s["summed"], 1)
                        return
                    for h in range(heads):
                        m = nc.tensor.matmul(psM[:, h, :], ends[:, mcol + h:mcol + h + 1].to_broadcast([P, P]),
                                             ident[:, :], start=True, stop=True)
                    m.then_inc(s["maxima"], 1)
                    pe.wait_ge(s["weights"], 1)
                    for h in range(heads):
                        m = nc.tensor.transpose(psV[:, h, :], val[:, h, :], ident[:, :])
                    m.then_inc(s["turned"], 1)
                    pe.wait_ge(s["valT"], 1)
                    for h in range(heads):
                        m = nc.tensor.matmul(psC[:, h * hw:(h + 1) * hw], valT[:, h, :], ends[:, h * hw:(h + 1) * hw],
                                             start=True, stop=True)
                    m.then_inc(s["summed"], 1)

        def node_pass(tag, layer=None, states=None, hidden=None, dense=None, width=D,
                      norm=None, table=None, relu=False):
            k = 1 if layer == 2 else 0
            sw = {0: W0, 1: D, 2: W2, 3: D, None: 1}[layer]
            soft = layer in (0, 2)
            heads = NH if layer == 2 else 1
            hw = {0: D + 1, 2: HD + 1}.get(layer)
            per = 512 // width
            tw = table.shape[1] if table is not None else 1
            with semaphores(nc) as sem, ExitStack() as ctx:
                def sb(n, shape, dt=F32):
                    return ctx.enter_context(nc.sbuf_tensor(f"{tag}_{n}", shape, dt))

                S = sb("S", [P, 2, GB, sw])
                ix = sb("ix", [P, 2, GB], I32)
                A = sb("A", [P, 2, GB, D])
                AT = sb("AT", [P, GB * P])
                HT = sb("HT", [P, GB * P])
                OB = sb("OB", [P, 2, GB, tw])
                den = sb("den", [P, GB, heads])
                R = sb("R", [P, 2, GB, D])
                st = sb("st", [P, GB, 6])
                mv = sb("mv", [P, GB, 2])
                sd = sb("sd", [P, GB])
                psT = ctx.enter_context(nc.psum_tensor(f"{tag}_psT", [P, 8 * P], F32))
                psH = ctx.enter_context(nc.psum_tensor(f"{tag}_psH", [P, 8 * P], F32))
                banks = -(-GB // per)
                psO = ctx.enter_context(nc.psum_tensor(f"{tag}_psO", [P, banks, 512], F32))
                s = {n: sem(f"{tag}_{n}") for n in (
                    "ix", "go", "A", "flipped", "AT", "hid", "HT", "out", "sunk",
                    "var", "std", "OB", "x", "queries", "spread")}
                if table is TKV:
                    queries = sb("queries", [P, NB, D])
                got = [sem(f"{tag}_got{h}") for h in range(2)]
                stored = [sem(f"{tag}_stored{h}") for h in range(2)]
                block = ctx.enter_context(nc.Block())

                def since(eng, sem, i, h, back):
                    if not (isinstance(i, int) and i * 2 + h < back):
                        eng.wait_ge(sem, i * 2 + h + 1 - back)

                def pieces():
                    for b in range(banks):
                        n = min(per, GB - b * per)
                        yield b * per, n, psO[:, b, 0:n * width].rearrange("p (j w) -> p j w", j=n)

                if layer is not None:
                    @block.gpsimd
                    def _(pool):
                        def step(i, h):
                            since(pool, s["A"], i, h, 2)
                            pool.wait_ge(s["ix"], i * 2 + h + 1)
                            pool.sem_inc(s["go"], 1)
                            for j in range(GB):
                                nc.gpsimd.indirect_dma_start(
                                    out=S[:, h, j, :], out_offset=None, in_=states[:, :],
                                    in_offset=bass.IndirectOffsetOnAxis(ap=ix[:, h, j:j + 1], axis=0)
                                ).then_inc(got[h], 16)

                        each(pool, GROUPS, 2, step)

                @block.scalar
                def _(act):
                    def step(i, h):
                        k0 = i * 2 + h
                        if layer is None:
                            since(act, s["flipped"], i, h, 2)
                            nc.scalar.copy(A[:, h], X[:, bass.ds(k0 * GB, GB), :]).then_inc(s["A"], 1)
                        if dense is not None:
                            act.wait_ge(s["flipped"], k0 + 1)
                            nc.scalar.copy(AT[:, :], psT[:, 0:GB * P]).then_inc(s["AT"], 1)
                        if hidden is not None:
                            act.wait_ge(s["hid"], k0 + 1)
                            nc.scalar.activation(HT[:, :], psH[:, 0:GB * P], ACT.Silu,
                                                 bias=hidden[1][:, 0:1]).then_inc(s["HT"], 1)
                        if norm is not None:
                            act.wait_ge(s["var"], k0 + 1)
                            nc.scalar.activation(sd[:, :], sd[:, :], ACT.Sqrt).then_inc(s["std"], 1)

                    each(act, GROUPS, 2, step)

                if table is TKV:
                    @block.gpsimd
                    def _(pool):
                        pool.wait_ge(s["queries"], 16)
                        for b in range(NB):
                            nc.gpsimd.indirect_dma_start(
                                out=QE[:, :], out_offset=bass.IndirectOffsetOnAxis(ap=startq[:, b:b + 1], axis=0),
                                in_=queries[:, b, :], in_offset=None).then_inc(s["spread"], 16)
                        nc.gpsimd.indirect_dma_start(
                            out=Qfirst[:, :], out_offset=None, in_=TQ[:, :],
                            in_offset=bass.IndirectOffsetOnAxis(ap=firstq[:, 0:1], axis=0)).then_inc(s["spread"], 16)
                        pool.wait_ge(s["spread"], 16 * (NB + 1))

                if dense is not None:
                    @block.tensor
                    def _(pe):
                        def step(i, h):
                            k0 = i * 2 + h
                            since(pe, s["AT"], i, h, 1)
                            pe.wait_ge(s["A"], k0 + 1)
                            for j in range(GB):
                                m = nc.tensor.transpose(psT[:, j * P:(j + 1) * P], A[:, h, j, :], ident[:, :])
                            m.then_inc(s["flipped"], 1)
                            cols = AT
                            if hidden is not None:
                                since(pe, s["HT"], i, h, 1)
                                pe.wait_ge(s["AT"], k0 + 1)
                                for c0, c1 in ((0, 512), (512, GB * P)):
                                    m = nc.tensor.matmul(psH[:, c0:c1], hidden[0][:, :], AT[:, c0:c1],
                                                         start=True, stop=True)
                                m.then_inc(s["hid"], 1)
                                cols = HT
                            since(pe, s["sunk"], i, h, 1)
                            pe.wait_ge(s["HT" if hidden is not None else "AT"], k0 + 1)
                            for b0, n, ps in pieces():
                                for j in range(n):
                                    at_ = (b0 + j) * P
                                    m = nc.tensor.matmul(ps[:, j, :], cols[:, at_:at_ + P], dense[0][:, :],
                                                         start=True, stop=True)
                            m.then_inc(s["out"], 1)

                        each(pe, GROUPS, 2, step)

                @block.vector
                def _(dve):
                    v = nc.vector
                    if table is not None:
                        v.memset(OB[:, :, :, :], 0.0)
                        v.drain()
                        if table is T0:
                            v.memset(OB[:, :, :, D:D + 1], 1.0)
                        if table is TKV:
                            for h in range(2):
                                v.memset(OB[:, h, :, D:].rearrange("p j (h d) -> p j h d", h=NH)[:, :, :, HD], 1.0)
                        v.drain()

                    def indices(i, h):
                        k0 = i * 2 + h
                        again(dve, got[h], i, 16 * GB)
                        v.tensor_copy(ix[:, h, :], endi[k][:, bass.ds(k0 * GB, GB)]).then_inc(s["ix"], 1)

                    def combine(i, h):
                        k0 = i * 2 + h
                        dve.wait_ge(got[h], 16 * GB * (i + 1))
                        if not (isinstance(i, int) and i * 2 + h + 2 >= GROUPS):
                            indices(i + 1, h)
                        if dense is not None:
                            since(dve, s["flipped"], i, h, 2)
                        hs = has[k][:, bass.ds(k0 * GB, GB)]
                        if not soft:
                            v.tensor_tensor(A[:, h], S[:, h], along(hs, D), ALU.mult).then_inc(s["A"], 1)
                            return
                        used = heads * hw
                        v.tensor_tensor(S[:, h, :, 0:used], S[:, h, :, 0:used], along(hs, used), ALU.mult)
                        v.drain()
                        w = S[:, h, :, 0:heads * hw].rearrange("p j (h d) -> p j h d", h=heads)
                        if layer == 0:
                            v.tensor_scalar(den[:, :, :], w[:, :, :, hw - 1], 1e-8, None, ALU.add)
                        else:
                            v.tensor_tensor(den[:, :, :], w[:, :, :, hw - 1], along(hs, heads), ALU.subtract)
                            v.drain()
                            v.tensor_scalar(den[:, :, :], den[:, :, :], 1.0, None, ALU.add)
                        v.drain()
                        v.reciprocal(den[:, :, :], den[:, :, :])
                        v.drain()
                        v.tensor_tensor(A[:, h].rearrange("p j (h d) -> p j h d", h=heads), w[:, :, :, 0:hw - 1],
                                        den[:, :, :].unsqueeze(3).to_broadcast([P, GB, heads, hw - 1]),
                                        ALU.mult).then_inc(s["A"], 1)
                        v.drain()

                    def sink(i, h):
                        k0 = i * 2 + h
                        xs = X[:, bass.ds(k0 * GB, GB), :]
                        if dense is not None:
                            dve.wait_ge(s["out"], k0 + 1)
                        if table is not None and norm is None:
                            again(dve, stored[h], i, 16)
                            for b0, n, ps in pieces():
                                js = slice(b0, b0 + n)
                                if table is T0:
                                    v.tensor_copy(OB[:, h, js, 0:D], ps[:, :, 0:D])
                                    v.tensor_copy(OB[:, h, js, D + 1:D + 2], ps[:, :, D:D + 1])
                                    m = v.tensor_copy(AD[:, bass.ds(k0 * GB + b0, n)], ps[:, :, D + 1])
                                elif table is TKV:
                                    v.tensor_tensor(OB[:, h, js, 0:D], ps[:, :, 0:D], over(dense[1][:, 0:D], n), ALU.add)
                                    for j in range(n):
                                        m = v.tensor_tensor(
                                            OB[:, h, b0 + j, D:].rearrange("p (h d) -> p h d", h=NH)[:, :, 0:HD],
                                            ps[:, j, D:2 * D].rearrange("p (h d) -> p h d", h=NH),
                                            dense[1][:, D:2 * D].rearrange("p (h d) -> p h d", h=NH), ALU.add)
                                elif relu:
                                    m = v.tensor_scalar(OB[:, h, js, :], ps, 0.0, None, ALU.max)
                                else:
                                    m = v.tensor_tensor(OB[:, h, js, :], ps, over(dense[1][:, :], n), ALU.add)
                            m.then_inc(s["sunk"], 1)
                            return
                        if norm == "out" or table is not None:
                            again(dve, stored[h], i, 16)
                        if dense is not None:
                            for b0, n, ps in pieces():
                                js = slice(b0, b0 + n)
                                m = v.tensor_tensor(R[:, h, js, :], ps, X[:, bass.ds(k0 * GB + b0, n), :], ALU.add)
                            m.then_inc(s["sunk"], 1)
                            if dense[1] is not None:
                                v.drain()
                                v.tensor_tensor(R[:, h], R[:, h], over(dense[1][:, :], GB), ALU.add)
                            if norm == "out":
                                v.drain()
                                v.tensor_tensor(R[:, h], R[:, h], xs, ALU.add)
                        else:
                            v.tensor_tensor(R[:, h], A[:, h], xs, ALU.add)
                        v.drain()
                        for j in range(GB):
                            v.bn_stats(st[:, j, :], R[:, h, j, :])
                        v.drain()
                        for j in range(GB):
                            v.bn_aggr(mv[:, j, :], st[:, j, :])
                        v.drain()
                        v.tensor_scalar(sd[:, :], mv[:, :, 1], 1e-5, None, ALU.add).then_inc(s["var"], 1)
                        dve.wait_ge(s["std"], k0 + 1)
                        v.reciprocal(sd[:, :], sd[:, :])
                        v.drain()
                        for j in range(GB):
                            m = v.tensor_scalar(R[:, h, j, :], R[:, h, j, :], mv[:, j, 0:1], sd[:, j:j + 1],
                                                ALU.subtract, ALU.mult)
                        if norm != "out":
                            v.drain()
                            m = v.tensor_copy(xs, R[:, h])
                        m.then_inc(s["x"], 1)
                        v.drain()

                    def step(i, h, last=False):
                        if layer is not None and not last:
                            i1, h1 = i + (h + 1) // 2, (h + 1) % 2
                            combine(i1, h1)
                        sink(i, h)

                    if layer is not None:
                        indices(0, 0)
                        indices(0, 1)
                        combine(0, 0)
                    each(dve, GROUPS - 1, 2, step)
                    step((GROUPS - 1) // 2, (GROUPS - 1) % 2, last=True)

                @block.sync
                def _(sp):
                    done = s["sunk"] if norm is None else s["x"]
                    if table is TKV:
                        sp.dma_start(queries[:, :, :], TQ.rearrange("(b p) f -> p b f", p=P)).then_inc(s["queries"], 16)

                    def step(i, h, last=False):
                        k0 = i * 2 + h
                        sp.wait_ge(done, k0 + 1)
                        of = R[:, h] if norm is not None else OB[:, h]
                        if norm == "out" and last:
                            b0 = (GROUPS - 1) * GB
                            sp.dma_start(out[b0 * P:(NB - 1) * P].rearrange("(b p) f -> p b f", p=P),
                                         of[:, 0:GB - 1, :]).then_inc(stored[h], 16)
                            sp.dma_start(out[(NB - 1) * P:N], of[0:N - (NB - 1) * P, GB - 1, :]).then_inc(stored[h], 16)
                        else:
                            to = out[0:(NB - 1) * P] if norm == "out" else table
                            sp.dma_start(to.rearrange("(b p) f -> p b f", p=P)[:, bass.ds(k0 * GB, GB), :],
                                         of).then_inc(stored[h], 16)

                    if table is not None or norm == "out":
                        each(sp, GROUPS - 1, 2, step)
                        step((GROUPS - 1) // 2, (GROUPS - 1) % 2, last=True)
                        sp.wait_ge(stored[0], 16 * (GROUPS // 2 + 1) + (16 if norm == "out" else 0))
                        sp.wait_ge(stored[1], 16 * (GROUPS // 2))

        with ExitStack() as early:
            inkeys = (early.enter_context(nc.sbuf_tensor("inputs", [P, NC, 4], F32)),
                      [early.enter_context(nc.sbuf_tensor(f"hi{k}", [P, NC], BF16)) for k in range(2)],
                      [early.enter_context(nc.sbuf_tensor(f"lo{k}", [P, NC], BF16)) for k in range(2)],
                      early.enter_context(nc.sbuf_tensor("scores", [P, NC, 2 + NH], F32)))
            setup(inkeys)
            count_edges(inkeys)
            sort_edges(inkeys, 1)
            with nc.If(nc.values_load(mixed[0:1, 0:1], min_val=0, max_val=1) > 0):
                sort_edges(inkeys, 0)
                take(0)
        node_pass("n0", dense=(w0, None), width=D + 2, table=T0)
        take(1)
        order_edges()
        spread_ad()
        edge_pass(0, "e0", T0, S0)
        carry_pass(0, "c0", S0)
        node_pass("f0", layer=0, states=S0, norm=True, table=T1)
        edge_pass(1, "e1", T1, S1)
        carry_pass(1, "c1", S1)
        node_pass("f1", layer=1, states=S1, dense=(w1[0], None), relu=True, table=TH)
        edge_pass(1, "e2", TH, S1)
        carry_pass(1, "c2", S1)
        node_pass("f2", layer=1, states=S1, dense=(w1[1], None), norm=True)
        node_pass("nq", dense=(wq, bq), table=TQ)
        node_pass("nk", dense=(wkv, bkv), width=2 * D, table=TKV)
        edge_pass(2, "e3", TKV, S2)
        carry_pass(2, "c3", S2)
        node_pass("f3", layer=2, states=S2, dense=(wo, bo), norm=True)
        node_pass("n3", hidden=(aw1, ab1), dense=(aw2, ab2), table=T3)
        edge_pass(3, "e4", T3, S1)
        carry_pass(3, "c4", S1)
        node_pass("f4", layer=3, states=S1, hidden=(ow1, ob1), dense=(ow2, ob2), norm="out")


_IN = ["x", "src", "dst", "edge_attr_128", "edge_attr_50", "edge_weight", "edge_weight_n2", "L0_gnn_W", "L0_gnn_a",
       "L1_gnn_W0", "L1_gnn_W1", "L2_gnn_Wq", "L2_gnn_bq", "L2_gnn_Wk", "L2_gnn_bk", "L2_gnn_Wv", "L2_gnn_bv",
       "L2_gnn_We", "L2_gnn_be", "L2_gnn_Wo", "L2_gnn_bo", "L3_gnn_fw1", "L3_gnn_fb1", "L3_gnn_fw2", "L3_gnn_fb2",
       "L3_gnn_aw1", "L3_gnn_ab1", "L3_gnn_aw2", "L3_gnn_ab2", "L3_gnn_ow1", "L3_gnn_ob1", "L3_gnn_ow2",
       "L3_gnn_ob2"]


def kernel(**inputs):
    import numpy as np
    import concourse.bacc as bacc
    from concourse.bass_utils import run_bass_kernel_spmd

    nc = bacc.Bacc("TRN2", target_bir_lowering=False, num_devices=1)
    arrays = {f"in_{n}": np.ascontiguousarray(inputs[n]) for n in _IN}
    t = {n: nc.dram_tensor(f"in_{n}", arrays[f"in_{n}"].shape, mybir.dt.from_np(arrays[f"in_{n}"].dtype),
                           kind="ExternalInput").ap() for n in _IN}
    out = nc.dram_tensor("out", (N, D), F32, kind="ExternalOutput").ap()
    gnn(nc, t, out)
    return run_bass_kernel_spmd(nc, [arrays], core_ids=[0]).results[0]["out"]
```
